# Optimizing a Trainium2 kernel written in Bass

```python
import numpy as np
import jax
import jax.numpy as jnp

def _softmax(x, axis=-1):
    return jax.nn.softmax(x, axis=axis)

def _gelu(x):
    return jax.nn.gelu(x, approximate=True)

def _silu(x):
    return jax.nn.silu(x)

def _sigmoid(x):
    return jax.nn.sigmoid(x)

def _layernorm(x, axis=-1, eps=1e-05):
    m = jnp.mean(x, axis=axis, keepdims=True)
    v = jnp.var(x, axis=axis, keepdims=True)
    return (x - m) / jnp.sqrt(v + eps)

def _scatter_add(tgt, idx, src, axis=0):
    return tgt.at[idx].add(src)

def _segment_sum(src, seg, n):
    return jax.ops.segment_sum(src, seg, n)
kernel_name = 'mk_seq_postln_d1_jaxref_r8_438e2a'

def setup_inputs(seed: int=0):
    np.random.seed(seed)
    _w = jnp.asarray

    def _L0_attn_setup():
        import jax, jax.numpy as jnp
        import numpy as np
        import math
        B, T, DIM, NH = (2, 256, 256, 16)
        HD = DIM // NH

        def rotate_half(x):
            h = x.shape[-1] // 2
            return jnp.concatenate([-x[..., h:], x[..., :h]], axis=-1)

        def rope_tables(t_len, rot_dim, base=10000.0, dtype=jnp.float32):
            inv_freq = 1.0 / base ** (jnp.arange(0, rot_dim, 2, dtype=dtype) / rot_dim)
            t = jnp.arange(t_len, dtype=dtype)
            ang = jnp.einsum('i,j->ij', t, inv_freq)
            return (jnp.sin(ang), jnp.cos(ang))

        def apply_rope(q, k, sin, cos):
            h = q.shape[-1] // 2
            q1, q2 = (q[..., :h], q[..., h:])
            k1, k2 = (k[..., :h], k[..., h:])
            sin = sin[None, None]
            cos = cos[None, None]
            q1r = q1 * cos + rotate_half(q1) * sin
            k1r = k1 * cos + rotate_half(k1) * sin
            return (jnp.concatenate([q1r, q2], axis=-1), jnp.concatenate([k1r, k2], axis=-1))
        key = jax.random.key(seed)
        ks = jax.random.split(key, 5)
        s = 1.0 / math.sqrt(DIM)
        return {'x': jax.random.normal(ks[0], (B, T, DIM), jnp.float32), 'wq': jax.random.normal(ks[1], (DIM, DIM), jnp.float32) * s, 'wk': jax.random.normal(ks[2], (DIM, DIM), jnp.float32) * s, 'wv': jax.random.normal(ks[3], (DIM, DIM), jnp.float32) * s, 'wo': jax.random.normal(ks[4], (DIM, DIM), jnp.float32) * s}
    _L0_attn_in = _L0_attn_setup()

    def _L0_ffn_setup():
        import jax, jax.numpy as jnp
        import numpy as np
        HIDDEN = 256
        INTER = 1024
        B, S = (4, 128)

        def _qmatmul(x, w_int8, scale):
            y = jnp.einsum('bsh,ho->bso', x, w_int8.astype(x.dtype))
            return y * scale
        key = jax.random.key(seed)
        ks = jax.random.split(key, 7)
        x = jax.random.normal(ks[0], (B, S, HIDDEN), dtype=jnp.float32)
        w_gate = jax.random.randint(ks[1], (HIDDEN, INTER), -128, 128, dtype=jnp.int32).astype(jnp.int8)
        w_up = jax.random.randint(ks[2], (HIDDEN, INTER), -128, 128, dtype=jnp.int32).astype(jnp.int8)
        w_down = jax.random.randint(ks[3], (INTER, HIDDEN), -128, 128, dtype=jnp.int32).astype(jnp.int8)
        s_gate = jax.random.uniform(ks[4], (INTER,), dtype=jnp.float32) * 0.02 + 0.001
        s_up = jax.random.uniform(ks[5], (INTER,), dtype=jnp.float32) * 0.02 + 0.001
        s_down = jax.random.uniform(ks[6], (HIDDEN,), dtype=jnp.float32) * 0.02 + 0.001
        return {'x': x, 'w_gate': w_gate, 'w_up': w_up, 'w_down': w_down, 's_gate': s_gate, 's_up': s_up, 's_down': s_down}
    _L0_ffn_in = _L0_ffn_setup()
    _d = {'L0_attn_x': _L0_attn_in['x'], 'L0_attn_wq': _L0_attn_in['wq'], 'L0_attn_wk': _L0_attn_in['wk'], 'L0_attn_wv': _L0_attn_in['wv'], 'L0_attn_wo': _L0_attn_in['wo'], 'L0_ffn_w_gate': _L0_ffn_in['w_gate'], 'L0_ffn_w_up': _L0_ffn_in['w_up'], 'L0_ffn_w_down': _L0_ffn_in['w_down'], 'L0_ffn_s_gate': _L0_ffn_in['s_gate'], 'L0_ffn_s_up': _L0_ffn_in['s_up'], 'L0_ffn_s_down': _L0_ffn_in['s_down']}
    _x0 = _d['L0_attn_x']
    _d['L0_attn_x'] = jax.random.normal(jax.random.fold_in(jax.random.key(seed), 1), (4, 1024, 256), dtype=_x0.dtype)
    del _x0
    return _d

def reference(L0_attn_x, L0_attn_wq, L0_attn_wk, L0_attn_wv, L0_attn_wo, L0_ffn_w_gate, L0_ffn_w_up, L0_ffn_w_down, L0_ffn_s_gate, L0_ffn_s_up, L0_ffn_s_down):

    def _L0_attn_ref(x, wq, wk, wv, wo):
        import jax, jax.numpy as jnp
        import numpy as np
        import math
        B, T, DIM, NH = (2, 256, 256, 16)
        HD = DIM // NH

        def rotate_half(x):
            h = x.shape[-1] // 2
            return jnp.concatenate([-x[..., h:], x[..., :h]], axis=-1)

        def rope_tables(t_len, rot_dim, base=10000.0, dtype=jnp.float32):
            inv_freq = 1.0 / base ** (jnp.arange(0, rot_dim, 2, dtype=dtype) / rot_dim)
            t = jnp.arange(t_len, dtype=dtype)
            ang = jnp.einsum('i,j->ij', t, inv_freq)
            return (jnp.sin(ang), jnp.cos(ang))

        def apply_rope(q, k, sin, cos):
            h = q.shape[-1] // 2
            q1, q2 = (q[..., :h], q[..., h:])
            k1, k2 = (k[..., :h], k[..., h:])
            sin = sin[None, None]
            cos = cos[None, None]
            q1r = q1 * cos + rotate_half(q1) * sin
            k1r = k1 * cos + rotate_half(k1) * sin
            return (jnp.concatenate([q1r, q2], axis=-1), jnp.concatenate([k1r, k2], axis=-1))
        b, t, c = x.shape

        def proj(w):
            return (x @ w.T).reshape(b, t, NH, HD).transpose(0, 2, 1, 3)
        q, k, v = (proj(wq), proj(wk), proj(wv))
        sin, cos = rope_tables(t, HD, dtype=x.dtype)
        q, k = apply_rope(q, k, sin, cos)
        att = jnp.einsum('bhqd,bhkd->bhqk', q, k) * (1.0 / math.sqrt(HD))
        att = jax.nn.softmax(att, axis=-1)
        y = jnp.einsum('bhqk,bhkd->bhqd', att, v)
        y = y.transpose(0, 2, 1, 3).reshape(b, t, c)
        return y @ wo.T

    def _L0_ffn_ref(x, w_gate, w_up, w_down, s_gate, s_up, s_down):
        import jax, jax.numpy as jnp
        import numpy as np
        HIDDEN = 256
        INTER = 1024
        B, S = (4, 128)

        def _qmatmul(x, w_int8, scale):
            y = jnp.einsum('bsh,ho->bso', x, w_int8.astype(x.dtype))
            return y * scale
        gate = jax.nn.silu(_qmatmul(x, w_gate, s_gate))
        up = _qmatmul(x, w_up, s_up)
        fuse = gate * up
        return _qmatmul(fuse, w_down, s_down)
    x = L0_attn_x
    x = _layernorm(x + _L0_attn_ref(x, L0_attn_wq, L0_attn_wk, L0_attn_wv, L0_attn_wo), axis=-1)
    x = _layernorm(x + _L0_ffn_ref(x, L0_ffn_w_gate, L0_ffn_w_up, L0_ffn_w_down, L0_ffn_s_gate, L0_ffn_s_up, L0_ffn_s_down), axis=-1)
    return x

_drawn_inputs = setup_inputs


def setup_inputs(seed=0):
    import zlib

    import numpy as np

    out = dict(_drawn_inputs(seed))
    spreads = {}
    factors = {}
    for name, (base, spread) in spreads.items():
        noise = np.random.default_rng([zlib.crc32(name.encode()), seed]).standard_normal(out[name].shape)
        drawn = base * np.exp(spread * noise) if base else spread * noise
        out[name] = jnp.asarray(drawn.astype(out[name].dtype))
    for name, factor in factors.items():
        out[name] = (out[name] * factor).astype(out[name].dtype)
    return out
```

```python
import concourse.bass as bass
from concourse import mybir
from contextlib import ExitStack


def build_attention_ffn_block(nc, x_nat, x_cols, w_qkv, w_out, rope_cos, rope_sin,
                              w_gate, w_up, w_down, s_gate, s_up, s_down, out):
    fp32, fp32r, bf16, i8 = mybir.dt.float32, mybir.dt.float32r, mybir.dt.bfloat16, mybir.dt.int8
    ALU, ACT, AX = mybir.AluOpType, mybir.ActivationFunctionType, mybir.AxisListType
    ds = bass.ds

    P = 128
    TOKENS, C = x_nat.shape
    BATCH = 4
    T = TOKENS // BATCH
    NH, HD = 16, 16
    HALF = HD // 2
    INTER = 4 * w_gate.shape[1]
    KC = C // P
    NB = 512
    CH = NB
    CHUNKS = TOKENS // CH
    TPC = CH // P
    G = 4
    GROUPS = BATCH * NH // G
    GPB = NH // G
    KT = T // P
    QC = T // CH
    PARTS = 3
    TERMS_Q, TERMS_K = (0, 0, 1, 0, 2, 1), (0, 1, 0, 2, 0, 1)
    NT = len(TERMS_Q)
    STACK = NT * HD
    SHIFT = STACK + PARTS
    SCALE = float(HD) ** -0.5
    OT = INTER // P
    EPS = 1e-5

    STEPS = 4 * KT
    BODIES = GROUPS // 2
    LEAD = 22
    MPC = G * TPC
    MPG = QC * MPC
    EPC = KT * G

    q_parts = nc.dram_tensor("q_parts", [BATCH * C, PARTS, T], bf16).ap()
    k_parts = nc.dram_tensor("k_parts", [BATCH * C, PARTS, T], bf16).ap()
    y_raw = nc.dram_tensor("y_raw", [BATCH * C, T], fp32).ap()
    row_sums = nc.dram_tensor("row_sums", [BATCH * NH, T], fp32).ap()
    row_rinv = nc.dram_tensor("row_rinv", [BATCH * NH, T], fp32).ap()

    ctx = ExitStack()
    with ctx:
        def sb_in(stack, name, shape, dt):
            return stack.enter_context(nc.sbuf_tensor(name, shape, dt))

        def sb(name, shape, dt):
            return sb_in(ctx, name, shape, dt)

        def sem(name):
            return ctx.enter_context(nc.semaphore(name))

        v_all = sb("v_all", [P, BATCH, GPB, KT, G * HD], fp32)
        wo_sb = sb("wo_sb", [P, KC, C], fp32)
        wg_sb = sb("wg_sb", [P, KC, INTER], fp32r)
        wu_sb = sb("wu_sb", [P, KC, INTER], fp32r)
        wd_sb = sb("wd_sb", [P, OT, C], fp32r)
        w8_sb = sb("w8_sb", [P, 3, KC * INTER // 4], mybir.dt.int32)
        sg_sb = sb("sg_sb", [P, OT], fp32)
        su_sb = sb("su_sb", [P, OT], fp32)
        sd_sb = sb("sd_sb", [P, C], fp32)
        neg_half = sb("neg_half", [P, TPC], fp32)
        ident_f = sb("ident_f", [P, P], fp32)
        ident_b = sb("ident_b", [P, P], bf16)

        with ExitStack() as p1:
            w_raw = sb_in(p1, "w_raw", [P, KC, 8 * P], fp32)
            w_hi = sb_in(p1, "w_hi", [P, KC, 8 * P], fp32r)
            w_lo = sb_in(p1, "w_lo", [P, KC, 8 * P], fp32r)
            cos_sb = sb_in(p1, "cos_sb", [P, T], fp32)
            sin_sb = sb_in(p1, "sin_sb", [P, T], fp32)
            x_raw = sb_in(p1, "x_raw", [P, 2, KC, CH], fp32)
            x_hi = [sb_in(p1, f"x_hi{s}", [P, KC, CH], fp32r) for s in range(2)]
            x_lo = [sb_in(p1, f"x_lo{s}", [P, KC, CH], fp32r) for s in range(2)]
            rope_a = sb_in(p1, "rope_a", [P, 2, CH], fp32)
            rope_r = sb_in(p1, "rope_r", [P, 2, CH], fp32)
            roped = sb_in(p1, "roped", [P, 2, CH], fp32)
            rest = sb_in(p1, "rest", [P, 4, CH], fp32)
            parts = sb_in(p1, "parts", [P, 4, PARTS, CH], bf16)

        with ExitStack() as p2:
            q_stack = [sb_in(p2, f"q_stack{p}", [SHIFT, QC, G, CH], bf16) for p in range(2)]
            k_stack = [sb_in(p2, f"k_stack{p}", [SHIFT, G, T], bf16) for p in range(2)]
            v_ones = [sb_in(p2, f"v_ones{p}", [P, KT, G, 2 * HD], fp32) for p in range(2)]
            probs = sb_in(p2, "probs", [P, 2, G, CH], fp32)
            mx = sb_in(p2, "mx", [P, 2, MPC], fp32)
            mx_rest = sb_in(p2, "mx_rest", [P, MPC], fp32)
            mx_parts = sb_in(p2, "mx_parts", [P, P], bf16)
            mx_rows = sb_in(p2, "mx_rows", [PARTS * MPC, P], bf16)
            o_sb = sb_in(p2, "o_sb", [P, 2, CH], fp32)
        sums_sb = sb("sums_sb", [P, BATCH * NH * T // P], fp32)
        y_in = sb("y_in", [P, KC, CH], fp32)
        r_in = sb("r_in", [P, KC, CH], fp32)
        x_in = sb("x_in", [P, TPC, C], fp32)
        y_n = sb("y_n", [P, KC, CH], fp32)
        res1 = sb("res1", [P, TPC, C], fp32)
        x1 = sb("x1", [P, TPC, C], fp32)
        x1_keep = sb("x1_keep", [P, 2, TPC, C], fp32)
        x1t_hi = sb("x1t_hi", [P, KC, CH], fp32r)
        x1t_lo = sb("x1t_lo", [P, KC, CH], fp32r)
        silu = sb("silu", [P, 2, CH], fp32)
        fused = sb("fused", [P, 2, CH], fp32)
        f_hi = sb("f_hi", [P, OT, CH], fp32r)
        f_lo = sb("f_lo", [P, OT, CH], fp32r)
        res2 = sb("res2", [P, TPC, C], fp32)
        out_sb = sb("out_sb", [P, TPC, C], fp32)
        st = sb("st", [P, 2, TPC, 6], fp32)
        ln_mean = sb("ln_mean", [P, 2, TPC], fp32)
        ln_diff = sb("ln_diff", [P, 2, TPC], fp32)
        ln_dev = sb("ln_dev", [P, 2, TPC], fp32)
        var_eps = sb("var_eps", [P, 2, TPC], fp32)
        rstd = sb("rstd", [P, 2, TPC], fp32)

        ps = ctx.enter_context(nc.psum_tensor("ps", [P, 8 * NB], fp32))
        bank = [ps[:, b * NB:(b + 1) * NB] for b in range(8)]
        score = bank[0:2]
        mscore = [ps[:, 2 * NB:4 * NB], ps[:, 4 * NB:6 * NB]]
        pv = bank[6]
        mx_t = bank[7].bitcast(bf16)
        mx_part = [mx_parts[:, k * MPC:(k + 1) * MPC] for k in range(PARTS)]
        ad_ps = ps[:, 0:2 * NB]
        b_ps = ps[:, 2 * NB:4 * NB]
        g_ps, u_ps = [bank[4], bank[6]], [bank[5], bank[7]]

        w_loaded, ffn_loaded = sem("w_loaded"), sem("ffn_loaded")
        x_loaded = [sem(f"x_loaded{s}") for s in range(2)]
        w_hi_done, w_lo_done = sem("w_hi_done"), sem("w_lo_done")
        x_hi_done, x_lo_done = sem("x_hi_done"), sem("x_lo_done")
        proj_done = sem("proj_done")
        p1_bank_free = [sem(f"p1_bank_free{b}") for b in range(8)]
        rope_terms = [sem(f"rope_terms{s}") for s in range(2)]
        rope_added = [sem(f"rope_added{s}") for s in range(2)]
        hi_done = [sem(f"hi_done{a}") for a in range(4)]
        rest_done = [sem(f"rest_done{a}") for a in range(4)]
        mid_done = [sem(f"mid_done{a}") for a in range(4)]
        lo_done = [sem(f"lo_done{a}") for a in range(4)]
        p1_bank_free[2], p1_bank_free[5] = rest_done[1], rest_done[3]
        parts_stored = [sem(f"parts_stored{a}") for a in range(4)]

        consts_done, ident0 = sem("consts_done"), sem("ident0")
        stack_loaded = [sem(f"stack_loaded{p}") for p in range(2)]
        ones_done = sem("ones_done")
        v_ready = sem("v_ready")
        mscore_full = sem("mscore_full")
        mscore_free = [sem(f"mscore_free{k}") for k in range(2)]
        mx_step, mx_split, mx_transposed = sem("mx_step"), sem("mx_split"), sem("mx_transposed")
        mx_copied, shift_loaded = sem("mx_copied"), sem("shift_loaded")
        score_full = sem("score_full")
        exp_done = [sem(f"exp_done{k}") for k in range(2)]
        pv_done, pv_free = sem("pv_done"), sem("pv_free")
        o_stored = [sem(f"o_stored{p}") for p in range(2)]

        sums_loaded, rinv_done, rinv_stored = sem("sums_loaded"), sem("rinv_done"), sem("rinv_stored")
        y_loaded, y_normed = sem("y_loaded"), sem("y_normed")
        a_done, attn_read = sem("a_done"), sem("attn_read")
        ln_step = [sem(f"ln_step{k}") for k in range(2)]
        var_ready = [sem(f"var_ready{k}") for k in range(2)]
        rstd_ready = [sem(f"rstd_ready{k}") for k in range(2)]
        x1_ready, x1_kept = sem("x1_ready"), sem("x1_kept")
        b_done, x1t_hi_done, x1t_ready = sem("b_done"), sem("x1t_hi_done"), sem("x1t_ready")
        ffn_cast = sem("ffn_cast")
        g_full, u_full = sem("g_full"), sem("u_full")
        silu_done = [sem(f"silu_done{k}") for k in range(2)]
        fused_done = [sem(f"fused_done{k}") for k in range(2)]
        f_hi_done = sem("f_hi_done")
        f_lo_done = [sem(f"f_lo_done{k}") for k in range(2)]
        d_done, down_read = sem("d_done"), sem("down_read")
        out_ready, out_stored = sem("out_ready"), sem("out_stored")

        PARTS_STORE = 16 * PARTS
        STACK_LOAD = 16 * (1 + QC) * NT
        SHIFT_LOAD = 16
        O_STORE = 16 * (G + 1)
        Y_LOAD = 16 * (KC + KC + 1)

        w_cols = ["qa", "qr", "qb", "ka", "kr", "kb"]
        block = ctx.enter_context(nc.Block())

        @block.sync
        def _(sp):
            sp.dma_start(w_raw[:, :, :], w_qkv.rearrange("(k p) n -> p k n", p=P)).then_inc(w_loaded, 16)

            def load_x(n, s):
                sp.dma_start(x_raw[:, s, :, :],
                             x_cols.rearrange("(k p) t -> p k t", p=P)[:, :, ds(n * CH, CH)])\
                  .then_inc(x_loaded[s], 16)

            load_x(0, 0)
            load_x(1, 1)
            sp.dma_start(cos_sb[:, :], rope_cos).then_inc(w_loaded, 16)
            sp.dma_start(sin_sb[:, :], rope_sin).then_inc(w_loaded, 16)

            def phase1(i, last):
                for s in range(2):
                    n = 2 * i + s
                    if not last:
                        sp.wait_ge(w_loaded, 48)
                        sp.wait_ge(x_lo_done, n + 1)
                        load_x(n + 2, s)
                    for a in (1, 0, 3, 2):
                        dst = (q_parts if a < 2 else k_parts)
                        rows = dst[ds(i * C, C), :, s * CH:(s + 1) * CH]\
                            .rearrange("(h j d) part t -> j h d part t", j=2, d=HALF)[a % 2]
                        sp.wait_ge(w_loaded, 48)
                        sp.wait_ge(lo_done[a], n + 1)
                        for part in range(PARTS):
                            sp.dma_start(rows[:, :, part, :], parts[:, a, part, :])\
                              .then_inc(parts_stored[a], 16)

            with sp.Fori(0, BATCH - 1) as i:
                phase1(i, False)
            phase1(BATCH - 1, True)

            for a in range(4):
                sp.wait_ge(parts_stored[a], PARTS_STORE * CHUNKS)
            sp.wait_ge(proj_done, 8 * CHUNKS)

            def load_stacks(g, p):
                group = ds(g * G * HD, G * HD)
                k_rows = k_parts[group, :, :].rearrange("(h d) part t -> d part h t", d=HD)
                q_rows = q_parts[group, :, :].rearrange("(h d) part (c t) -> d part c h t", d=HD, c=QC)
                for t in range(NT):
                    rows = slice(t * HD, (t + 1) * HD)
                    sp.dma_start(k_stack[p][rows, :, :], k_rows[:, TERMS_K[t], :, :]).then_inc(stack_loaded[p], 16)
                    for qc in range(QC):
                        sp.dma_start(q_stack[p][rows, qc, :, :], q_rows[:, TERMS_Q[t], qc, :, :])\
                          .then_inc(stack_loaded[p], 16)

            def load_shift(c, rc):
                p, qc = (rc // QC) % 2, rc % QC
                sp.wait_ge(mx_copied, c + 1)
                sp.dma_start(q_stack[p][STACK:SHIFT, qc, :, :].rearrange("a h q -> a (h q)"), mx_rows[:, :])\
                  .then_inc(shift_loaded, 16)

            def store_o(i, k):
                c, p, qc = 4 * i + k, k % 2, k % QC
                g = 2 * i + k // QC
                sp.wait_ge(w_loaded, 48)
                sp.wait_ge(pv_free, c + 1)
                for h in range(G):
                    sp.dma_start(y_raw[ds(g * G * HD + h * HD, HD), qc * CH:(qc + 1) * CH],
                                 o_sb[2 * HD * h:2 * HD * h + HD, p, :]).then_inc(o_stored[p], 16)
                sp.dma_start(row_sums[ds(g * G, G), qc * CH:(qc + 1) * CH],
                             o_sb[HD:P:2 * HD, p, :]).then_inc(o_stored[p], 16)

            load_stacks(0, 0)
            for n, w in enumerate((w_gate, w_up)):
                sp.dma_start(w8_sb[:, n, :].rearrange("p (k o) -> p k o", k=KC),
                             w.rearrange("(k p) o -> p k o", p=P)).then_inc(ffn_loaded, 16)
            sp.dma_start(w8_sb[:, 2, :].rearrange("p (k o) -> p k o", k=OT),
                         w_down.rearrange("(k p) o -> p k o", p=P)).then_inc(ffn_loaded, 16)
            sp.dma_start(wo_sb[:, :, :], w_out.rearrange("(k p) o -> p k o", p=P)).then_inc(ffn_loaded, 16)
            sp.dma_start(sg_sb[:, :], s_gate).then_inc(ffn_loaded, 16)
            sp.dma_start(su_sb[:, :], s_up).then_inc(ffn_loaded, 16)
            sp.dma_start(sd_sb[:, :], s_down.unsqueeze(0).to_broadcast([P, C])).then_inc(ffn_loaded, 16)
            load_shift(0, 0)

            def phase2(i, last):
                sp.wait_ge(w_loaded, 48)
                sp.wait_ge(score_full, 2 * QC * EPC * i)
                load_stacks(2 * i + 1, 1)
                load_shift(4 * i + 1, 1)
                store_o(i, 0)
                load_shift(4 * i + 2, 2)
                if not last:
                    sp.wait_ge(w_loaded, 48)
                    sp.wait_ge(score_full, 2 * QC * EPC * i + QC * EPC)
                    load_stacks(2 * i + 2, 0)
                store_o(i, 1)
                load_shift(4 * i + 3, 3)
                store_o(i, 2)
                if not last:
                    load_shift(4 * i + 4, 4)
                store_o(i, 3)

            with sp.Fori(0, BODIES - 1) as i:
                phase2(i, False)
            phase2(BODIES - 1, True)

            for p in range(2):
                sp.wait_ge(o_stored[p], O_STORE * GROUPS)
            sp.dma_start(sums_sb[:, :], row_sums.rearrange("r (a t) -> (r a) t", a=P // (BATCH * NH)))\
              .then_inc(sums_loaded, 16)
            sp.wait_ge(rinv_done, 1)
            sp.dma_start(row_rinv.rearrange("r (a t) -> (r a) t", a=P // (BATCH * NH)), sums_sb[:, :])\
              .then_inc(rinv_stored, 16)
            sp.wait_ge(rinv_stored, 16)

            def load_chunk(n):
                b, cols = n // 2, (n % 2) * CH
                for k in range(KC):
                    sp.dma_start(y_in[:, k, :], y_raw[ds(b * C + k * P, P), ds(cols, CH)])\
                      .then_inc(y_loaded, 16)
                    sp.dma_start(r_in[:, k, :],
                                 row_rinv[ds(b * NH + k * (P // HD), P // HD), ds(cols, CH)]
                                 .unsqueeze(1).to_broadcast([P // HD, HD, CH]))\
                      .then_inc(y_loaded, 16)
                sp.dma_start(x_in[:, :, :],
                             x_nat[ds(n * CH, CH), :].rearrange("(t p) c -> p t c", p=P))\
                  .then_inc(y_loaded, 16)

            load_chunk(0)

            def phase3(n, last):
                if not last:
                    sp.wait_ge(w_loaded, 48)
                    sp.wait_ge(y_normed, n + 1)
                    sp.wait_ge(attn_read, n + 1)
                    load_chunk(n + 1)
                sp.wait_ge(w_loaded, 48)
                sp.wait_ge(out_ready, TPC * (n + 1))
                sp.dma_start(out[ds(n * CH, CH), :].rearrange("(t p) c -> p t c", p=P), out_sb[:, :, :])\
                  .then_inc(out_stored, 16)

            with sp.Fori(0, CHUNKS - 1) as n:
                phase3(n, False)
            phase3(CHUNKS - 1, True)
            sp.wait_ge(out_stored, 16 * CHUNKS)

        @block.tensor
        def _(pe):
            pe.wait_ge(w_lo_done, 1)

            def phase1(i):
                for s in range(2):
                    n = 2 * i + s
                    pe.wait_ge(x_lo_done, n + 1)
                    for b in range(6):
                        pe.wait_ge(p1_bank_free[b], n)
                        passes = [(w, x, k) for w, x in ((w_hi, x_hi[s]), (w_hi, x_lo[s]), (w_lo, x_hi[s]))
                                  for k in range(KC)]
                        for m, (w, x, k) in enumerate(passes):
                            ins = nc.tensor.matmul(bank[b], w[:, k, b * P:(b + 1) * P], x[:, k, :],
                                                   start=(m == 0), stop=(m == len(passes) - 1))
                        ins.then_inc(proj_done, 1)
                    for v in range(2):
                        pe.wait_ge(p1_bank_free[6 + v], n)
                        for t in range(2):
                            tile = slice((2 * v + t) * P, (2 * v + t + 1) * P)
                            passes = [(w, x, k) for w, x in ((w_hi, x_hi[s]), (w_lo, x_hi[s]), (w_hi, x_lo[s]))
                                      for k in range(KC)]
                            for m, (w, x, k) in enumerate(passes):
                                ins = nc.tensor.matmul(bank[6 + v][:, t * C:(t + 1) * C], x[:, k, tile],
                                                       w[:, k, 6 * P:8 * P],
                                                       start=(m == 0), stop=(m == len(passes) - 1))
                        ins.then_inc(proj_done, 1)

            with pe.Fori(0, BATCH) as i:
                phase1(i)

            for b in range(8):
                pe.wait_ge(p1_bank_free[b], CHUNKS)

            def max_scores(i, r, half):
                p, rg = (r // MPG) % 2, r % MPG
                qc, h, qt = rg // MPC, (rg % MPC) // TPC, rg % TPC
                if half == 0:
                    pe.wait_ge(mscore_free[r % 2], MPG * i + r // 2)
                ins = nc.tensor.matmul(mscore[r % 2][:, half * NB:(half + 1) * NB],
                                       q_stack[p][0:STACK, qc, h, qt * P:(qt + 1) * P],
                                       k_stack[p][0:STACK, h, half * NB:(half + 1) * NB],
                                       start=True, stop=True)
                if half == 1:
                    ins.then_inc(mscore_full, 1)

            def scores(t, rt, h):
                p, qc, kt = (rt // (QC * KT)) % 2, (rt // KT) % QC, rt % KT
                pe.wait_ge(exp_done[h % 2], 2 * t + h // 2)
                nc.tensor.matmul(score[h % 2], k_stack[p][0:SHIFT, h, kt * P:(kt + 1) * P],
                                 q_stack[p][0:SHIFT, qc, h, :],
                                 start=True, stop=True).then_inc(score_full, 1)

            def times_v(t, rt):
                p, kt = (rt // (QC * KT)) % 2, rt % KT
                for k in range(2):
                    pe.wait_ge(exp_done[k], 2 * (t + 1))
                for h in range(G):
                    ins = nc.tensor.matmul(pv[2 * HD * h:2 * HD * (h + 1), :], v_ones[p][:, kt, h, :],
                                           probs[:, rt % 2, h, :], start=(kt == 0), stop=(kt == KT - 1),
                                           skip_group_check=True)
                ins.then_inc(pv_done, 1)

            def transpose_max(c):
                pe.wait_ge(mx_split, c + 1)
                pe.wait_ge(mx_copied, c)
                nc.tensor.transpose(mx_t[:, 0:P], mx_parts[:, :], ident_b[:, :]).then_inc(mx_transposed, 1)

            pe.wait_ge(consts_done, 2)
            pe.wait_ge(stack_loaded[0], STACK_LOAD)
            for r in range(LEAD):
                for half in range(2):
                    max_scores(0, r, half)
            transpose_max(0)
            pe.wait_ge(ones_done, 4)
            pe.wait_ge(shift_loaded, SHIFT_LOAD)
            for h in range(G):
                scores(0, 0, h)

            def phase2(i, last):
                for j in range(STEPS):
                    t = STEPS * i + j
                    if (j + 1) % KT == 0 and not (last and j == STEPS - 1):
                        pe.wait_ge(shift_loaded, SHIFT_LOAD * (4 * i + (j + 1) // KT + 1))
                    for h in range(G):
                        if not (last and j == STEPS - 1):
                            scores(t + 1, j + 1, h)
                        r = 2 * j + LEAD + h // 2
                        if last and r >= 2 * MPG:
                            continue
                        if r % MPG == 0 and h % 2 == 0:
                            p = (r // MPG) % 2
                            pe.wait_ge(stack_loaded[p], STACK_LOAD * (i + 1 + (r // MPG) // 2))
                        max_scores(i, r, h % 2)
                    if j % KT == 0:
                        pe.wait_ge(pv_free, 4 * i + j // KT)
                    if j % (QC * KT) == 0:
                        pe.wait_ge(v_ready, 2 * i + j // (QC * KT) + 1)
                    times_v(t, j)
                    if j % KT == 5 and not (last and j == STEPS - 3):
                        transpose_max(4 * i + j // KT + 1)

            with pe.Fori(0, BODIES - 1) as i:
                phase2(i, False)
            phase2(BODIES - 1, True)

            for k in range(2):
                pe.wait_ge(exp_done[k], GROUPS * QC * EPC // 2)
                pe.wait_ge(mscore_free[k], GROUPS * MPG // 2)
            pe.wait_ge(pv_free, GROUPS * QC)
            pe.wait_ge(mx_copied, GROUPS * QC)
            pe.wait_ge(ffn_cast, 3)

            def attn_out(m):
                pe.wait_ge(y_normed, m + 1)
                for t in range(TPC):
                    for k in range(KC):
                        ins = nc.tensor.matmul(ad_ps[:, t * C:(t + 1) * C], y_n[:, k, t * P:(t + 1) * P],
                                               wo_sb[:, k, :], start=(k == 0), stop=(k == KC - 1))
                ins.then_inc(a_done, 1)

            def transpose_x1(m):
                pe.wait_ge(x1_ready, m + 1)
                pe.wait_ge(x1t_ready, m)
                for k in range(KC):
                    for t in range(TPC):
                        ins = nc.tensor.transpose(b_ps[:, k * CH + t * P:k * CH + (t + 1) * P],
                                                  x1[:, t, k * P:(k + 1) * P], ident_f[:, :])
                ins.then_inc(b_done, 1)

            def gate_up(n, o):
                cols = slice(o * P, (o + 1) * P)
                for acc, w, freed, full in ((g_ps[o % 2], wg_sb, silu_done[o % 2], g_full),
                                            (u_ps[o % 2], wu_sb, fused_done[o % 2], u_full)):
                    pe.wait_ge(freed, OT // 2 * n + o // 2)
                    passes = [(x, k) for x in (x1t_hi, x1t_lo) for k in range(KC)]
                    for m, (x, k) in enumerate(passes):
                        ins = nc.tensor.matmul(acc, w[:, k, cols], x[:, k, :],
                                               start=(m == 0), stop=(m == len(passes) - 1))
                    ins.then_inc(full, 1)

            def down(n):
                for k in range(2):
                    pe.wait_ge(f_lo_done[k], OT // 2 * (n + 1))
                for t in range(TPC):
                    passes = [(f, o) for f in (f_hi, f_lo) for o in range(OT)]
                    for m, (f, o) in enumerate(passes):
                        ins = nc.tensor.matmul(ad_ps[:, t * C:(t + 1) * C], f[:, o, t * P:(t + 1) * P],
                                               wd_sb[:, o, :], start=(m == 0), stop=(m == len(passes) - 1))
                ins.then_inc(d_done, 1)

            attn_out(0)
            transpose_x1(0)

            def phase3(n, last):
                pe.wait_ge(x1t_ready, n + 1)
                for o in range(OT // 2):
                    gate_up(n, o)
                if not last:
                    pe.wait_ge(down_read, n)
                    attn_out(n + 1)
                for o in range(OT // 2, OT):
                    gate_up(n, o)
                if not last:
                    transpose_x1(n + 1)
                pe.wait_ge(attn_read, n + 1 if last else n + 2)
                down(n)

            with pe.Fori(0, CHUNKS - 1) as n:
                phase3(n, False)
            phase3(CHUNKS - 1, True)

        @block.scalar
        def _(act):
            act.wait_ge(w_loaded, 48)
            nc.scalar.activation(w_hi[:, :, :], w_raw[:, :, :], ACT.Copy).then_inc(w_hi_done, 1)

            def x_high(n, i, s):
                act.wait_ge(x_loaded[s], 16 * (i + 1))
                nc.scalar.activation(x_hi[s][:, :, :], x_raw[:, s, :, :], ACT.Copy).then_inc(x_hi_done, 1)

            x_high(0, 0, 0)
            x_high(1, 0, 1)

            def phase1(i, last):
                for s in range(2):
                    n = 2 * i + s
                    for side in range(2):
                        b = 3 * side + 2
                        act.wait_ge(proj_done, 8 * n + b + 1)
                        act.wait_ge(parts_stored[2 * side + 1], PARTS_STORE * n)
                        nc.scalar.activation(parts[:, 2 * side + 1, 0, :], bank[b], ACT.Copy)\
                          .then_inc(hi_done[2 * side + 1], 1)
                        act.wait_ge(rope_added[side], n + 1)
                        act.wait_ge(parts_stored[2 * side], PARTS_STORE * n)
                        nc.scalar.activation(parts[:, 2 * side, 0, :], roped[:, side, :], ACT.Copy)\
                          .then_inc(hi_done[2 * side], 1)
                    for v in range(2):
                        act.wait_ge(proj_done, 8 * n + 7 + v)
                        for t in range(2):
                            ins = nc.scalar.activation(
                                v_all[:, ds(i, 1), :, s * TPC + 2 * v + t, :].rearrange("p a g d -> p (a g) d"),
                                bank[6 + v][:, t * C:(t + 1) * C].rearrange("p (g d) -> p g d", g=GPB), ACT.Copy)
                        ins.then_inc(p1_bank_free[6 + v], 1)
                    if not last:
                        act.wait_ge(proj_done, 8 * n + 8)
                        x_high(n + 2, i + 1, s)

            with act.Fori(0, BATCH - 1) as i:
                phase1(i, False)
            phase1(BATCH - 1, True)

            def exps(t, rt):
                for h in range(G):
                    act.wait_ge(score_full, G * t + h + 1)
                    nc.scalar.activation(probs[:, rt % 2, h, :], score[h % 2], ACT.Exp, scale=SCALE)\
                      .then_inc(exp_done[h % 2], 1)

            exps(0, 0)

            def phase2(i, last):
                for j in range(STEPS):
                    t = STEPS * i + j
                    if not (last and j == STEPS - 1):
                        act.wait_ge(pv_done, t)
                        exps(t + 1, j + 1)
                    if j % KT == KT - 1:
                        k = j // KT
                        act.wait_ge(pv_done, t + 1)
                        act.wait_ge(o_stored[k % 2], O_STORE * (2 * i + k // 2))
                        nc.scalar.activation(o_sb[:, k % 2, :], pv, ACT.Copy).then_inc(pv_free, 1)

            with act.Fori(0, BODIES - 1) as i:
                phase2(i, False)
            phase2(BODIES - 1, True)

            def x1t_high(m):
                act.wait_ge(b_done, m + 1)
                nc.scalar.activation(x1t_hi[:, :, :], b_ps.rearrange("p (k t) -> p k t", k=KC), ACT.Copy)\
                  .then_inc(x1t_hi_done, 1)

            def silu_gate(n, o):
                act.wait_ge(g_full, OT * n + o + 1)
                act.wait_ge(fused_done[o % 2], OT // 2 * n + o // 2)
                nc.scalar.activation(silu[:, o % 2, :], g_ps[o % 2], ACT.Silu, scale=sg_sb[:, o:o + 1])\
                  .then_inc(silu_done[o % 2], 1)

            def fused_high(n, o):
                act.wait_ge(fused_done[o % 2], OT // 2 * n + o // 2 + 1)
                nc.scalar.activation(f_hi[:, o, :], fused[:, o % 2, :], ACT.Copy).then_inc(f_hi_done, 1)

            act.wait_ge(ffn_loaded, 16 * 7)
            x1t_high(0)

            def phase3(n, last):
                silu_gate(n, 0)
                act.wait_ge(d_done, n)
                for o in range(1, OT):
                    silu_gate(n, o)
                    fused_high(n, o - 1)
                fused_high(n, OT - 1)
                if not last:
                    x1t_high(n + 1)

            with act.Fori(0, CHUNKS - 1) as n:
                phase3(n, False)
            phase3(CHUNKS - 1, True)

        @block.vector
        def _(dve):
            dve.wait_ge(w_hi_done, 1)
            nc.vector.tensor_tensor(w_lo[:, :, :], w_raw[:, :, :], w_hi[:, :, :].bitcast(fp32), ALU.subtract)\
              .then_inc(w_lo_done, 1)
            dve.wait_ge(w_loaded, 48)

            def phase1(i):
                for s in range(2):
                    n = 2 * i + s
                    cols = slice(s * CH, (s + 1) * CH)

                    def rope(side):
                        b = 3 * side
                        dve.wait_ge(proj_done, 8 * n + b + 2)
                        dve.wait_ge(rope_added[side], n)
                        nc.vector.tensor_tensor(rope_a[:, side, :], bank[b], cos_sb[:, cols], ALU.mult)\
                          .then_inc(p1_bank_free[b], 1)
                        nc.vector.tensor_tensor(rope_r[:, side, :], bank[b + 1], sin_sb[:, cols], ALU.mult)\
                          .then_inc(p1_bank_free[b + 1], 1)

                    def take_rest(a):
                        dve.wait_ge(hi_done[a], n + 1)
                        dve.wait_ge(mid_done[a], n)
                        side = a // 2
                        src = bank[3 * side + 2] if a % 2 else roped[:, side, :]
                        ins = nc.vector.tensor_tensor(rest[:, a, :], src, parts[:, a, 0, :], ALU.subtract)
                        ins.then_inc(rest_done[a], 1)

                    def low(a):
                        dve.wait_ge(mid_done[a], n + 1)
                        nc.vector.tensor_tensor(parts[:, a, 2, :], rest[:, a, :], parts[:, a, 1, :],
                                                ALU.subtract).then_inc(lo_done[a], 1)

                    rope(0)
                    take_rest(1)
                    rope(1)
                    take_rest(0)
                    low(1)
                    take_rest(3)
                    low(0)
                    take_rest(2)
                    low(3)
                    low(2)

            with dve.Fori(0, BATCH) as i:
                phase1(i)

            def row_max(i, r):
                dve.wait_ge(mscore_full, 2 * MPG * i + r + 1)
                nc.vector.tensor_reduce(out=mx[:, (r // MPC) % 2, r % MPC:r % MPC + 1], in_=mscore[r % 2],
                                        axis=AX.X, op=ALU.max).then_inc(mscore_free[r % 2], 1)

            def split_max(c, rc):
                m = mx[:, rc % 2, :]
                for k in range(2):
                    dve.wait_ge(mscore_free[k], MPC // 2 * (c + 1))
                nc.vector.tensor_scalar(mx_part[0], m, -1.0, None, ALU.mult).then_inc(mx_step, 1)
                dve.wait_ge(mx_step, 3 * c + 1)
                nc.vector.scalar_tensor_tensor(out=mx_rest[:, :], in0=m, scalar=-1.0, in1=mx_part[0],
                                               op0=ALU.mult, op1=ALU.subtract).then_inc(mx_step, 1)
                dve.wait_ge(mx_step, 3 * c + 2)
                nc.vector.tensor_copy(mx_part[1], mx_rest[:, :]).then_inc(mx_step, 1)
                dve.wait_ge(mx_step, 3 * c + 3)
                nc.vector.tensor_tensor(mx_part[2], mx_rest[:, :], mx_part[1], ALU.subtract)\
                  .then_inc(mx_split, 1)

            def copy_rows(c):
                dve.wait_ge(mx_transposed, c + 1)
                dve.wait_ge(shift_loaded, SHIFT_LOAD * c)
                nc.vector.tensor_copy(mx_rows[:, :], mx_t[0:PARTS * MPC, 0:P]).then_inc(mx_copied, 1)

            dve.wait_ge(mscore_full, 1)
            nc.vector.memset(mx_parts[:, PARTS * MPC:P], 0.0)
            for r in range(MPC):
                row_max(0, r)
            split_max(0, 0)
            for r in range(MPC, LEAD):
                row_max(0, r)
            copy_rows(0)

            def phase2(i, last):
                for j in range(STEPS):
                    for r in (2 * j + LEAD, 2 * j + LEAD + 1):
                        if not (last and r >= 2 * MPG):
                            row_max(i, r)
                    if not (last and j // KT == STEPS // KT - 1):
                        if j % KT == 4:
                            split_max(4 * i + j // KT + 1, j // KT + 1)
                        if j % KT == 5:
                            copy_rows(4 * i + j // KT + 1)

            with dve.Fori(0, BODIES - 1) as i:
                phase2(i, False)
            phase2(BODIES - 1, True)

            dve.wait_ge(sums_loaded, 16)
            nc.vector.reciprocal(sums_sb[:, :], sums_sb[:, :]).then_inc(rinv_done, 1)

            def layernorm(m, k, step, steps, src, dst, done):
                def stepped(ins, at):
                    ins.then_inc(ln_step[k], 1)
                    dve.wait_ge(ln_step[k], steps * m + step + at)

                for t in range(TPC):
                    ins = nc.vector.bn_stats(st[:, k, t, :], src[:, t, :])
                stepped(ins, 1)
                mean_e, dev_e, mean_o, dev_o = (st[:, k, :, c] for c in (1, 2, 4, 5))
                nc.vector.tensor_tensor(ln_mean[:, k, :], mean_e, mean_o, ALU.add)
                nc.vector.tensor_tensor(ln_diff[:, k, :], mean_e, mean_o, ALU.subtract)
                stepped(nc.vector.tensor_tensor(ln_dev[:, k, :], dev_e, dev_o, ALU.add), 2)
                nc.vector.tensor_scalar(ln_mean[:, k, :], ln_mean[:, k, :], 0.5, None, ALU.mult)
                nc.vector.tensor_scalar(ln_dev[:, k, :], ln_dev[:, k, :], 1.0 / C, EPS, ALU.mult, ALU.add)
                stepped(nc.vector.scalar_tensor_tensor(out=ln_diff[:, k, :], in0=ln_diff[:, k, :], scalar=0.25,
                                                       in1=ln_diff[:, k, :], op0=ALU.mult, op1=ALU.mult), 3)
                nc.vector.tensor_tensor(var_eps[:, k, :], ln_dev[:, k, :], ln_diff[:, k, :], ALU.add)\
                  .then_inc(var_ready[k], 1)
                dve.wait_ge(rstd_ready[k], m + 1)
                for t in range(TPC):
                    ins = nc.vector.tensor_scalar(dst[:, t, :], src[:, t, :], ln_mean[:, k, t:t + 1],
                                                  rstd[:, k, t:t + 1], ALU.subtract, ALU.mult)
                    if k == 1 or t == TPC - 1:
                        ins.then_inc(done, 1)

            def layernorm1(m):
                dve.wait_ge(a_done, m + 1)
                dve.wait_ge(y_loaded, Y_LOAD * (m + 1))
                nc.vector.tensor_tensor(res1[:, :, :], ad_ps.rearrange("p (t c) -> p t c", c=C), x_in[:, :, :],
                                        ALU.add).then_inc(attn_read, 1)
                dve.wait_ge(attn_read, m + 1)
                dve.wait_ge(b_done, m)
                dve.wait_ge(x1_kept, m)
                layernorm(m, 0, 0, 3, res1, x1, x1_ready)

            def layernorm2(m, keep):
                dve.wait_ge(d_done, m + 1)
                nc.vector.tensor_tensor(res2[:, :, :], ad_ps.rearrange("p (t c) -> p t c", c=C),
                                        sd_sb[:, :].unsqueeze(1).to_broadcast([P, TPC, C]), ALU.mult)\
                  .then_inc(down_read, 1)
                dve.wait_ge(down_read, m + 1)
                dve.wait_ge(x1_kept, m + 1)
                nc.vector.tensor_tensor(res2[:, :, :], res2[:, :, :], keep, ALU.add).then_inc(ln_step[1], 1)
                dve.wait_ge(ln_step[1], 4 * m + 1)
                dve.wait_ge(out_stored, 16 * m)
                layernorm(m, 1, 1, 4, res2, out_sb, out_ready)

            def fuse(n, o):
                dve.wait_ge(u_full, OT * n + o + 1)
                dve.wait_ge(silu_done[o % 2], OT // 2 * n + o // 2 + 1)
                dve.wait_ge(f_lo_done[o % 2], OT // 2 * n + o // 2)
                nc.vector.scalar_tensor_tensor(out=fused[:, o % 2, :], in0=u_ps[o % 2], scalar=su_sb[:, o:o + 1],
                                               in1=silu[:, o % 2, :], op0=ALU.mult, op1=ALU.mult)\
                  .then_inc(fused_done[o % 2], 1)

            def x1t_low(m):
                dve.wait_ge(x1t_hi_done, m + 1)
                nc.vector.tensor_tensor(x1t_lo[:, :, :], b_ps.rearrange("p (k t) -> p k t", k=KC),
                                        x1t_hi[:, :, :].bitcast(fp32), ALU.subtract).then_inc(x1t_ready, 1)

            dve.wait_ge(ffn_loaded, 16 * 7)
            layernorm1(0)
            x1t_low(0)

            def phase3(n, last):
                for o in range(OT // 2):
                    fuse(n, o)
                if not last:
                    layernorm1(n + 1)
                for o in range(OT // 2, OT):
                    fuse(n, o)
                if not last:
                    x1t_low(n + 1)
                keep = x1_keep[:, ds(n % 2, 1), :, :].rearrange("p a t c -> p (a t) c")
                layernorm2(n, keep)

            with dve.Fori(0, CHUNKS - 1) as n:
                phase3(n, False)
            phase3(CHUNKS - 1, True)

        @block.gpsimd
        def _(pool):
            nc.gpsimd.memset(ident_f[:, :], 0.0).then_inc(ident0, 1)
            nc.gpsimd.memset(ident_b[:, :], 0.0).then_inc(ident0, 1)
            nc.gpsimd.memset(neg_half[:, :], -0.5).then_inc(ident0, 1)
            pool.wait_ge(ident0, 3)
            nc.gpsimd.affine_select(out=ident_f[:, :], in_=ident_f[:, :], compare_op=ALU.not_equal, fill=1.0,
                                    base=0, pattern=[[-1, P]], channel_multiplier=1).then_inc(consts_done, 1)
            nc.gpsimd.affine_select(out=ident_b[:, :], in_=ident_b[:, :], compare_op=ALU.not_equal, fill=1.0,
                                    base=0, pattern=[[-1, P]], channel_multiplier=1).then_inc(consts_done, 1)

            def x_low(n, s):
                pool.wait_ge(x_hi_done, n + 1)
                nc.gpsimd.tensor_tensor(x_lo[s][:, :, :], x_raw[:, s, :, :], x_hi[s][:, :, :].bitcast(fp32),
                                        ALU.subtract).then_inc(x_lo_done, 1)

            x_low(0, 0)
            x_low(1, 1)

            def phase1(i, last):
                for s in range(2):
                    n = 2 * i + s

                    def add_rope(side):
                        pool.wait_ge(p1_bank_free[3 * side], n + 1)
                        pool.wait_ge(p1_bank_free[3 * side + 1], n + 1)
                        pool.wait_ge(rest_done[2 * side], n)
                        nc.gpsimd.tensor_tensor(roped[:, side, :], rope_a[:, side, :], rope_r[:, side, :],
                                                ALU.add).then_inc(rope_added[side], 1)

                    def middle(a):
                        pool.wait_ge(ident0, 3)
                        pool.wait_ge(rest_done[a], n + 1)
                        nc.gpsimd.tensor_copy(parts[:, a, 1, :], rest[:, a, :]).then_inc(mid_done[a], 1)

                    add_rope(0)
                    middle(1)
                    add_rope(1)
                    middle(0)
                    middle(3)
                    middle(2)
                    if not last:
                        x_low(n + 2, s)

            with pool.Fori(0, BATCH - 1) as i:
                phase1(i, False)
            phase1(BATCH - 1, True)

            pool.wait_ge(proj_done, 8 * CHUNKS)
            for a in range(4):
                pool.wait_ge(parts_stored[a], PARTS_STORE * CHUNKS)
            for v in range(2):
                pool.wait_ge(p1_bank_free[6 + v], CHUNKS)
            for n, ones in enumerate((k_stack[0][STACK:SHIFT, :, :], v_ones[0][:, :, :, :],
                                      k_stack[1][STACK:SHIFT, :, :], v_ones[1][:, :, :, :])):
                nc.gpsimd.memset(ones, 1.0).then_inc(ones_done, 1)
                pool.wait_ge(ones_done, n + 1)

            def place_v(g, b, hg, p):
                nc.gpsimd.tensor_copy(
                    v_ones[p][:, :, :, 0:HD],
                    v_all[:, ds(b, 1), ds(hg, 1), :, :].rearrange("p a b k (h d) -> p (a b k) h d", d=HD))\
                  .then_inc(v_ready, 1)

            place_v(0, 0, 0, 0)
            pool.wait_ge(ffn_loaded, 16 * 7)
            for w, n, k in ((wg_sb, 0, KC), (wu_sb, 1, KC), (wd_sb, 2, OT)):
                nc.gpsimd.tensor_copy(w[:, :, :], w8_sb[:, n, :].bitcast(i8).rearrange("p (k o) -> p k o", k=k))\
                  .then_inc(ffn_cast, 1)

            def phase2(i, last):
                g = 2 * i + 1
                pool.wait_ge(ones_done, 4)
                pool.wait_ge(pv_done, STEPS * i)
                place_v(g, g // GPB, g % GPB, 1)
                if not last:
                    g = 2 * i + 2
                    pool.wait_ge(ones_done, 4)
                    pool.wait_ge(pv_done, STEPS * i + STEPS // 2)
                    place_v(g, g // GPB, g % GPB, 0)

            with pool.Fori(0, BODIES - 1) as i:
                phase2(i, False)
            phase2(BODIES - 1, True)

            pool.wait_ge(ident0, 3)

            def norm_y(m):
                pool.wait_ge(y_loaded, Y_LOAD * (m + 1))
                pool.wait_ge(a_done, m)
                nc.gpsimd.tensor_tensor(y_n[:, :, :], y_in[:, :, :], r_in[:, :, :], ALU.mult).then_inc(y_normed, 1)

            def root(m, k):
                pool.wait_ge(var_ready[k], m + 1)
                nc.gpsimd.tensor_tensor(rstd[:, k, :], var_eps[:, k, :], neg_half[:, :], ALU.pow)\
                  .then_inc(rstd_ready[k], 1)

            def keep_x1(m):
                pool.wait_ge(x1_ready, m + 1)
                nc.gpsimd.tensor_copy(x1_keep[:, ds(m % 2, 1), :, :].rearrange("p a t c -> p (a t) c"),
                                      x1[:, :, :]).then_inc(x1_kept, 1)

            def fused_low(n, o):
                pool.wait_ge(f_hi_done, OT * n + o + 1)
                nc.gpsimd.tensor_tensor(f_lo[:, o, :], fused[:, o % 2, :], f_hi[:, o, :].bitcast(fp32),
                                        ALU.subtract).then_inc(f_lo_done[o % 2], 1)

            norm_y(0)
            root(0, 0)
            keep_x1(0)

            def phase3(n, last):
                if not last:
                    norm_y(n + 1)
                for o in range(OT // 2):
                    fused_low(n, o)
                if not last:
                    root(n + 1, 0)
                    pool.wait_ge(ident0, 3)
                    pool.wait_ge(ln_step[1], 4 * n)
                    keep_x1(n + 1)
                for o in range(OT // 2, OT):
                    fused_low(n, o)
                root(n, 1)

            with pool.Fori(0, CHUNKS - 1) as n:
                phase3(n, False)
            phase3(CHUNKS - 1, True)


def kernel(**inputs):
    import numpy as np
    import concourse.bacc as bacc
    from concourse import mybir
    from concourse.bass_utils import run_bass_kernel_spmd

    HEADS, HD, HALF, T = 16, 16, 8, 1024
    x = np.asarray(inputs["L0_attn_x"])
    B, _, C = x.shape
    x_nat = np.ascontiguousarray(x.reshape(B * T, C))
    heads = np.arange(HEADS)[:, None] * HD
    d = np.arange(HALF)[None, :]
    rotary = (heads + d).ravel()
    partner = (heads + (d + HALF // 2) % HALF).ravel()
    plain = (heads + HALF + d).ravel()
    wq, wk, wv, wo = (np.asarray(inputs[f"L0_attn_{n}"]) for n in ("wq", "wk", "wv", "wo"))
    w_qkv = np.ascontiguousarray(np.concatenate(
        [wq.T[:, rotary], wq.T[:, partner], wq.T[:, plain],
         wk.T[:, rotary], wk.T[:, partner], wk.T[:, plain], wv.T], axis=1))
    inv_freq = (1.0 / np.float32(10000.0) ** (np.arange(0, HD, 2, dtype=np.float32) / np.float32(HD))).astype(np.float32)
    angle = inv_freq[:, None] * np.arange(T, dtype=np.float32)[None, :]
    sign = np.where(np.arange(HALF) < HALF // 2, -1.0, 1.0).astype(np.float32)[:, None]
    cos = np.tile(np.cos(angle), (HEADS, 1)).astype(np.float32)
    sin = np.tile(sign * np.sin(angle), (HEADS, 1)).astype(np.float32)
    arrays = {
        "x_nat": x_nat,
        "x_cols": np.ascontiguousarray(x_nat.T),
        "w_qkv": w_qkv,
        "w_out": np.ascontiguousarray(wo.T),
        "rope_cos": cos,
        "rope_sin": sin,
    }
    for name in ("w_gate", "w_up", "w_down", "s_gate", "s_up", "s_down"):
        arrays[name] = np.ascontiguousarray(np.asarray(inputs[f"L0_ffn_{name}"]))
    for name in ("w_gate", "w_up", "w_down"):
        arrays[name] = arrays[name].view(np.int32)
    for name in ("s_gate", "s_up"):
        arrays[name] = np.ascontiguousarray(arrays[name].reshape(-1, 128).T)
    nc = bacc.Bacc("TRN2", target_bir_lowering=False, num_devices=1)
    args = [nc.dram_tensor(n, a.shape, mybir.dt.from_np(a.dtype), kind="ExternalInput").ap()
            for n, a in arrays.items()]
    out = nc.dram_tensor("out", (B * T, C), mybir.dt.float32, kind="ExternalOutput").ap()
    build_attention_ffn_block(nc, *args, out)
    r = run_bass_kernel_spmd(nc, [arrays], core_ids=[0])
    return r.results[0]["out"].reshape(B, T, C)
```

```python
import concourse.bass as bass
from concourse import mybir
from contextlib import ExitStack


def build_attention_ffn_block(nc, x_nat, x_cols, w_qkv, w_out, rope_cos, rope_sin,
                              w_gate, w_up, w_down, s_gate, s_up, s_down, out):
    fp32, fp32r, bf16, i8 = mybir.dt.float32, mybir.dt.float32r, mybir.dt.bfloat16, mybir.dt.int8
    ALU, ACT, AX = mybir.AluOpType, mybir.ActivationFunctionType, mybir.AxisListType
    ds = bass.ds

    P = 128
    TOKENS, C = x_nat.shape
    BATCH = 4
    T = TOKENS // BATCH
    NH, HD = 16, 16
    HALF = HD // 2
    INTER = 4 * w_gate.shape[1]
    KC = C // P
    NB = 512
    CH = NB
    CHUNKS = TOKENS // CH
    TPC = CH // P
    G = 4
    GROUPS = BATCH * NH // G
    GPB = NH // G
    KT = T // P
    QC = T // CH
    PARTS = 3
    TERMS_Q, TERMS_K = (0, 0, 1, 0, 2, 1), (0, 1, 0, 2, 0, 1)
    NT = len(TERMS_Q)
    STACK = NT * HD
    SHIFT = STACK + PARTS
    SCALE = float(HD) ** -0.5
    OT = INTER // P
    EPS = 1e-5

    STEPS = 4 * KT
    BODIES = GROUPS // 2
    LEAD = 24
    MPC = G * TPC
    MPG = QC * MPC
    EPC = KT * G

    q_parts = nc.dram_tensor("q_parts", [BATCH * C, PARTS, T], bf16).ap()
    k_parts = nc.dram_tensor("k_parts", [BATCH * C, PARTS, T], bf16).ap()
    y_raw = nc.dram_tensor("y_raw", [BATCH * C, T], fp32).ap()
    row_sums = nc.dram_tensor("row_sums", [BATCH * NH, T], fp32).ap()
    row_rinv = nc.dram_tensor("row_rinv", [BATCH * NH, T], fp32).ap()

    ctx = ExitStack()
    with ctx:
        def sb_in(stack, name, shape, dt):
            return stack.enter_context(nc.sbuf_tensor(name, shape, dt))

        def sb(name, shape, dt):
            return sb_in(ctx, name, shape, dt)

        def sem(name):
            return ctx.enter_context(nc.semaphore(name))

        v_all = sb("v_all", [P, BATCH, GPB, KT, G * HD], fp32)
        wo_sb = sb("wo_sb", [P, KC, C], fp32)
        wg_sb = sb("wg_sb", [P, KC, INTER], fp32r)
        wu_sb = sb("wu_sb", [P, KC, INTER], fp32r)
        wd_sb = sb("wd_sb", [P, OT, C], fp32r)
        sg_sb = sb("sg_sb", [P, OT], fp32)
        su_sb = sb("su_sb", [P, OT], fp32)
        sd_sb = sb("sd_sb", [P, C], fp32)
        neg_half = sb("neg_half", [P, TPC], fp32)
        ident_f = sb("ident_f", [P, P], fp32)
        ident_b = sb("ident_b", [P, P], bf16)

        with ExitStack() as late:
            f_hi = [sb_in(late, f"f_hi{s}", [P, OT, CH], fp32r) for s in range(2)]
            f_lo = [sb_in(late, f"f_lo{s}", [P, OT, CH], fp32r) for s in range(2)]

        q_stack = [sb(f"q_stack{p}", [SHIFT, QC, G, CH], bf16) for p in range(2)]
        k_stack = [sb(f"k_stack{p}", [SHIFT, G, T], bf16) for p in range(2)]
        v_ones = [sb(f"v_ones{p}", [P, KT, G, 2 * HD], fp32) for p in range(2)]
        with ExitStack() as raw:
            w_raw = sb_in(raw, "w_raw", [P, KC, 8 * P], fp32)
            x_raw = sb_in(raw, "x_raw", [P, 2, KC, CH], fp32)
        probs = sb("probs", [P, 2, G, CH], fp32)
        mx = sb("mx", [P, 2, MPC], fp32)
        mx_rest = sb("mx_rest", [P, MPC], fp32)
        mx_parts = sb("mx_parts", [P, P], bf16)
        mx_rows = sb("mx_rows", [PARTS * MPC, P], bf16)
        o_sb = sb("o_sb", [P, 2, CH], fp32)
        w8_sb = sb("w8_sb", [P, 3, KC * INTER // 4], mybir.dt.int32)

        with ExitStack() as p1:
            w_hi = sb_in(p1, "w_hi", [P, KC, 8 * P], fp32r)
            w_lo = sb_in(p1, "w_lo", [P, KC, 8 * P], fp32r)
            cos_sb = sb_in(p1, "cos_sb", [P, T], fp32)
            sin_sb = sb_in(p1, "sin_sb", [P, T], fp32)
            x_hi = [sb_in(p1, f"x_hi{s}", [P, KC, CH], fp32r) for s in range(2)]
            x_lo = [sb_in(p1, f"x_lo{s}", [P, KC, CH], fp32r) for s in range(2)]
            rope_a = sb_in(p1, "rope_a", [P, 2, CH], fp32)
            rope_r = sb_in(p1, "rope_r", [P, 2, CH], fp32)
            roped = sb_in(p1, "roped", [P, 2, CH], fp32)
            rest = sb_in(p1, "rest", [P, 4, CH], fp32)
            parts = sb_in(p1, "parts", [P, 4, PARTS, CH], bf16)

        sums_sb = sb("sums_sb", [P, BATCH, NH * T // P], fp32)
        y_in = sb("y_in", [P, KC, CH], fp32)
        r_in = sb("r_in", [P, KC, CH], fp32)
        x_in = sb("x_in", [P, TPC, C], fp32)
        y_n = sb("y_n", [P, KC, CH], fp32)
        res1 = sb("res1", [P, TPC, C], fp32)
        x1 = [sb(f"x1_{s}", [P, TPC, C], fp32) for s in range(2)]
        x1t_hi = [sb(f"x1t_hi{s}", [P, KC, CH], fp32r) for s in range(2)]
        x1t_lo = [sb(f"x1t_lo{s}", [P, KC, CH], fp32r) for s in range(2)]
        silu = sb("silu", [P, 2, CH], fp32)
        fused = sb("fused", [P, 2, CH], fp32)
        res2 = sb("res2", [P, TPC, C], fp32)
        out_sb = sb("out_sb", [P, TPC, C], fp32)
        st = sb("st", [P, 2, TPC, 6], fp32)
        ln_mean = sb("ln_mean", [P, 2, TPC], fp32)
        ln_diff = sb("ln_diff", [P, 2, TPC], fp32)
        ln_dev = sb("ln_dev", [P, 2, TPC], fp32)
        var_eps = sb("var_eps", [P, 2, TPC], fp32)
        rstd = sb("rstd", [P, 2, TPC], fp32)

        ps = ctx.enter_context(nc.psum_tensor("ps", [P, 8 * NB], fp32))
        bank = [ps[:, b * NB:(b + 1) * NB] for b in range(8)]
        score = bank[0:2]
        mscore = [ps[:, 2 * NB:4 * NB], ps[:, 4 * NB:6 * NB]]
        pv = bank[6]
        mx_t = bank[7].bitcast(bf16)
        mx_part = [mx_parts[:, k * MPC:(k + 1) * MPC] for k in range(PARTS)]
        ad_ps = ps[:, 0:2 * NB]
        b_ps = ps[:, 2 * NB:4 * NB]
        g_ps, u_ps = [bank[4], bank[6]], [bank[5], bank[7]]

        w_loaded = [sem(f"w_loaded{n}") for n in range(3)]
        tables_loaded, ffn_loaded = sem("tables_loaded"), sem("ffn_loaded")
        x_loaded = [sem(f"x_loaded{s}") for s in range(2)]
        w_hi_done, w_lo_done = sem("w_hi_done"), sem("w_lo_done")
        x_hi_done, x_lo_done = sem("x_hi_done"), sem("x_lo_done")
        proj_done = sem("proj_done")
        p1_bank_free = [sem(f"p1_bank_free{b}") for b in range(8)]
        rope_terms = [sem(f"rope_terms{s}") for s in range(2)]
        rope_added = [sem(f"rope_added{s}") for s in range(2)]
        hi_done = [sem(f"hi_done{a}") for a in range(4)]
        rest_done = [sem(f"rest_done{a}") for a in range(4)]
        mid_done = [sem(f"mid_done{a}") for a in range(4)]
        lo_done = [sem(f"lo_done{a}") for a in range(4)]
        p1_bank_free[2], p1_bank_free[5] = rest_done[1], rest_done[3]
        parts_stored = [sem(f"parts_stored{a}") for a in range(4)]

        consts_done, ident0 = sem("consts_done"), sem("ident0")
        stack_loaded = [sem(f"stack_loaded{p}") for p in range(2)]
        ones_done = sem("ones_done")
        v_ready = sem("v_ready")
        mscore_full = sem("mscore_full")
        mscore_free = [sem(f"mscore_free{k}") for k in range(2)]
        mx_step, mx_split, mx_transposed = sem("mx_step"), sem("mx_split"), sem("mx_transposed")
        mx_copied, shift_loaded = sem("mx_copied"), sem("shift_loaded")
        score_full = sem("score_full")
        exp_done = [sem(f"exp_done{k}") for k in range(2)]
        pv_done, pv_free = sem("pv_done"), sem("pv_free")
        o_stored = [sem(f"o_stored{p}") for p in range(2)]

        sums_loaded = [sem(f"sums_loaded{k}") for k in range(2)]
        rinv_stored = [sem(f"rinv_stored{k}") for k in range(2)]
        rinv_done = sem("rinv_done")
        y_loaded, y_normed = sem("y_loaded"), sem("y_normed")
        a_done, attn_read = sem("a_done"), sem("attn_read")
        ln_step = [sem(f"ln_step{k}") for k in range(2)]
        var_ready = [sem(f"var_ready{k}") for k in range(2)]
        rstd_ready = [sem(f"rstd_ready{k}") for k in range(2)]
        x1_ready = sem("x1_ready")
        b_done, x1t_hi_done, x1t_ready = sem("b_done"), sem("x1t_hi_done"), sem("x1t_ready")
        ffn_cast = sem("ffn_cast")
        g_full, u_full = sem("g_full"), sem("u_full")
        silu_done = [sem(f"silu_done{k}") for k in range(2)]
        fused_done = [sem(f"fused_done{k}") for k in range(2)]
        f_hi_done = sem("f_hi_done")
        f_lo_done = [sem(f"f_lo_done{k}") for k in range(2)]
        d_done, down_read = sem("d_done"), sem("down_read")
        out_ready, out_stored = sem("out_ready"), sem("out_stored")

        START = 1
        from_start = [*p1_bank_free[:2], *p1_bank_free[3:5], *p1_bank_free[6:], *rest_done, *rope_added,
                      *mid_done, *parts_stored, score_full, pv_done, pv_free, *o_stored, *silu_done,
                      *fused_done, d_done, down_read, *f_lo_done, out_stored]

        PARTS_STORE = 16 * PARTS
        STACK_LOAD = 16 * (1 + QC) * NT
        SHIFT_LOAD = 16
        O_STORE = 16 * (G + 1)
        Y_LOAD = 16 * (KC + KC + 1)

        w_piece = [slice(0, 3 * P), slice(3 * P, 6 * P), slice(6 * P, 8 * P)]
        block = ctx.enter_context(nc.Block())

        @block.sync
        def _(sp):
            def load_x(n, s):
                sp.dma_start(x_raw[:, s, :, :],
                             x_cols.rearrange("(k p) t -> p k t", p=P)[:, :, ds(n * CH, CH)])\
                  .then_inc(x_loaded[s], 16)

            def load_w(n):
                sp.dma_start(w_raw[:, :, w_piece[n]], w_qkv.rearrange("(k p) n -> p k n", p=P)[:, :, w_piece[n]])\
                  .then_inc(w_loaded[n], 16)

            load_x(0, 0)
            load_w(0)
            sp.dma_start(cos_sb[:, :], rope_cos).then_inc(tables_loaded, 16)
            sp.dma_start(sin_sb[:, :], rope_sin).then_inc(tables_loaded, 16)
            load_w(1)
            load_w(2)
            load_x(1, 1)

            def phase1(i, last):
                for s in range(2):
                    n = 2 * i + s
                    if not last:
                        sp.wait_ge(x_loaded[0], 16)
                        sp.wait_ge(x_lo_done, n + 1)
                        load_x(n + 2, s)
                    for a in (1, 0, 3, 2):
                        dst = (q_parts if a < 2 else k_parts)
                        rows = dst[ds(i * C, C), :, s * CH:(s + 1) * CH]\
                            .rearrange("(h j d) part t -> j h d part t", j=2, d=HALF)[a % 2]
                        sp.wait_ge(x_loaded[0], 16)
                        sp.wait_ge(lo_done[a], n + 1)
                        for part in range(PARTS):
                            sp.dma_start(rows[:, :, part, :], parts[:, a, part, :])\
                              .then_inc(parts_stored[a], 16)

            def load_stacks(g, p):
                group = ds(g * G * HD, G * HD)
                k_rows = k_parts[group, :, :].rearrange("(h d) part t -> d part h t", d=HD)
                q_rows = q_parts[group, :, :].rearrange("(h d) part (c t) -> d part c h t", d=HD, c=QC)
                for t in range(NT):
                    rows = slice(t * HD, (t + 1) * HD)
                    sp.dma_start(k_stack[p][rows, :, :], k_rows[:, TERMS_K[t], :, :]).then_inc(stack_loaded[p], 16)
                    for qc in range(QC):
                        sp.dma_start(q_stack[p][rows, qc, :, :], q_rows[:, TERMS_Q[t], qc, :, :])\
                          .then_inc(stack_loaded[p], 16)

            with sp.Fori(0, BATCH - 1) as i:
                phase1(i, False)
            for a in range(4):
                sp.wait_ge(parts_stored[a], START + PARTS_STORE * QC)
            load_stacks(0, 0)
            phase1(BATCH - 1, True)

            def load_shift(c, rc):
                p, qc = (rc // QC) % 2, rc % QC
                sp.wait_ge(mx_copied, c + 1)
                sp.dma_start(q_stack[p][STACK:SHIFT, qc, :, :].rearrange("a h q -> a (h q)"), mx_rows[:, :])\
                  .then_inc(shift_loaded, 16)

            def store_o(i, k):
                c, p, qc = 4 * i + k, k % 2, k % QC
                g = 2 * i + k // QC
                sp.wait_ge(x_loaded[0], 16)
                sp.wait_ge(pv_free, START + c + 1)
                for h in range(G):
                    sp.dma_start(y_raw[ds(g * G * HD + h * HD, HD), qc * CH:(qc + 1) * CH],
                                 o_sb[2 * HD * h:2 * HD * h + HD, p, :]).then_inc(o_stored[p], 16)
                sp.dma_start(row_sums[ds(g * G, G), qc * CH:(qc + 1) * CH],
                             o_sb[HD:P:2 * HD, p, :]).then_inc(o_stored[p], 16)

            for n, w in enumerate((w_gate, w_up)):
                sp.dma_start(w8_sb[:, n, :].rearrange("p (k o) -> p k o", k=KC),
                             w.rearrange("(k p) o -> p k o", p=P)).then_inc(ffn_loaded, 16)
            sp.dma_start(w8_sb[:, 2, :].rearrange("p (k o) -> p k o", k=OT),
                         w_down.rearrange("(k p) o -> p k o", p=P)).then_inc(ffn_loaded, 16)
            sp.dma_start(wo_sb[:, :, :], w_out.rearrange("(k p) o -> p k o", p=P)).then_inc(ffn_loaded, 16)
            sp.dma_start(sg_sb[:, :], s_gate).then_inc(ffn_loaded, 16)
            sp.dma_start(su_sb[:, :], s_up).then_inc(ffn_loaded, 16)
            sp.dma_start(sd_sb[:, :], s_down.unsqueeze(0).to_broadcast([P, C])).then_inc(ffn_loaded, 16)

            for a in range(4):
                sp.wait_ge(parts_stored[a], START + PARTS_STORE * CHUNKS)
            load_shift(0, 0)

            def invert_sums(batch, count):
                for b in range(batch, batch + count):
                    sp.dma_start(sums_sb[:, b, :], row_sums[b * NH:(b + 1) * NH, :]
                                 .rearrange("r (a t) -> (r a) t", a=P // NH)).then_inc(sums_loaded[b // 3], 16)
                sp.wait_ge(rinv_done, batch + count)
                for b in range(batch, batch + count):
                    sp.dma_start(row_rinv[b * NH:(b + 1) * NH, :].rearrange("r (a t) -> (r a) t", a=P // NH),
                                 sums_sb[:, b, :]).then_inc(rinv_stored[b // 3], 16)

            def load_chunk(n):
                b, cols = n // 2, (n % 2) * CH
                for k in range(KC):
                    sp.dma_start(y_in[:, k, :], y_raw[ds(b * C + k * P, P), ds(cols, CH)])\
                      .then_inc(y_loaded, 16)
                    sp.dma_start(r_in[:, k, :],
                                 row_rinv[ds(b * NH + k * (P // HD), P // HD), ds(cols, CH)]
                                 .unsqueeze(1).to_broadcast([P // HD, HD, CH]))\
                      .then_inc(y_loaded, 16)
                sp.dma_start(x_in[:, :, :],
                             x_nat[ds(n * CH, CH), :].rearrange("(t p) c -> p t c", p=P))\
                  .then_inc(y_loaded, 16)

            def phase2(i, last):
                sp.wait_ge(x_loaded[0], 16)
                sp.wait_ge(score_full, START + 2 * QC * EPC * i)
                load_stacks(2 * i + 1, 1)
                load_shift(4 * i + 1, 1)
                store_o(i, 0)
                load_shift(4 * i + 2, 2)
                if not last:
                    sp.wait_ge(x_loaded[0], 16)
                    sp.wait_ge(score_full, START + 2 * QC * EPC * i + QC * EPC)
                    load_stacks(2 * i + 2, 0)
                store_o(i, 1)
                load_shift(4 * i + 3, 3)
                if last:
                    for p in range(2):
                        sp.wait_ge(o_stored[p], START + O_STORE * 3 * GPB)
                    invert_sums(0, 3)
                store_o(i, 2)
                if not last:
                    load_shift(4 * i + 4, 4)
                else:
                    sp.wait_ge(rinv_stored[0], 16 * 3)
                    load_chunk(0)
                store_o(i, 3)

            with sp.Fori(0, BODIES - 1) as i:
                phase2(i, False)
            phase2(BODIES - 1, True)

            sp.wait_ge(y_normed, 1)
            sp.wait_ge(attn_read, 1)
            load_chunk(1)
            for p in range(2):
                sp.wait_ge(o_stored[p], START + O_STORE * GROUPS)
            invert_sums(3, 1)
            sp.wait_ge(rinv_stored[1], 16)

            def phase3(n):
                if not (isinstance(n, int) and n + 2 >= CHUNKS):
                    sp.wait_ge(x_loaded[0], 16)
                    sp.wait_ge(y_normed, n + 2)
                    sp.wait_ge(attn_read, n + 2)
                    load_chunk(n + 2)
                sp.wait_ge(x_loaded[0], 16)
                sp.wait_ge(out_ready, TPC * (n + 1))
                sp.dma_start(out[ds(n * CH, CH), :].rearrange("(t p) c -> p t c", p=P), out_sb[:, :, :])\
                  .then_inc(out_stored, 16)

            with sp.Fori(0, CHUNKS - 2) as n:
                phase3(n)
            for n in (CHUNKS - 2, CHUNKS - 1):
                phase3(n)
            sp.wait_ge(out_stored, START + 16 * CHUNKS)

        @block.tensor
        def _(pe):
            def phase1(i):
                for s in range(2):
                    n = 2 * i + s
                    pe.wait_ge(x_lo_done, n + 1)
                    for b in range(6):
                        if b % 3 == 0:
                            pe.wait_ge(w_lo_done, b // 3 + 1)
                        pe.wait_ge(p1_bank_free[b], START + n)
                        passes = [(w, x, k) for w, x in ((w_hi, x_hi[s]), (w_hi, x_lo[s]), (w_lo, x_hi[s]))
                                  for k in range(KC)]
                        for m, (w, x, k) in enumerate(passes):
                            ins = nc.tensor.matmul(bank[b], w[:, k, b * P:(b + 1) * P], x[:, k, :],
                                                   start=(m == 0), stop=(m == len(passes) - 1))
                        ins.then_inc(proj_done, 1)
                    pe.wait_ge(w_lo_done, 3)
                    for v in range(2):
                        pe.wait_ge(p1_bank_free[6 + v], START + n)
                        for t in range(2):
                            tile = slice((2 * v + t) * P, (2 * v + t + 1) * P)
                            passes = [(w, x, k) for w, x in ((w_hi, x_hi[s]), (w_lo, x_hi[s]), (w_hi, x_lo[s]))
                                      for k in range(KC)]
                            for m, (w, x, k) in enumerate(passes):
                                ins = nc.tensor.matmul(bank[6 + v][:, t * C:(t + 1) * C], x[:, k, tile],
                                                       w[:, k, 6 * P:8 * P],
                                                       start=(m == 0), stop=(m == len(passes) - 1))
                        ins.then_inc(proj_done, 1)

            with pe.Fori(0, BATCH) as i:
                phase1(i)

            for b in range(8):
                pe.wait_ge(p1_bank_free[b], START + CHUNKS)

            def max_scores(i, r, half):
                p, rg = (r // MPG) % 2, r % MPG
                qc, h, qt = rg // MPC, (rg % MPC) // TPC, rg % TPC
                if half == 0:
                    pe.wait_ge(mscore_free[r % 2], MPG * i + r // 2)
                ins = nc.tensor.matmul(mscore[r % 2][:, half * NB:(half + 1) * NB],
                                       q_stack[p][0:STACK, qc, h, qt * P:(qt + 1) * P],
                                       k_stack[p][0:STACK, h, half * NB:(half + 1) * NB],
                                       start=True, stop=True)
                if half == 1:
                    ins.then_inc(mscore_full, 1)

            def scores(t, rt, h):
                p, qc, kt = (rt // (QC * KT)) % 2, (rt // KT) % QC, rt % KT
                pe.wait_ge(exp_done[h % 2], 2 * t + h // 2)
                nc.tensor.matmul(score[h % 2], k_stack[p][0:SHIFT, h, kt * P:(kt + 1) * P],
                                 q_stack[p][0:SHIFT, qc, h, :],
                                 start=True, stop=True).then_inc(score_full, 1)

            def times_v(t, rt):
                p, kt = (rt // (QC * KT)) % 2, rt % KT
                for k in range(2):
                    pe.wait_ge(exp_done[k], 2 * (t + 1))
                for h in range(G):
                    ins = nc.tensor.matmul(pv[2 * HD * h:2 * HD * (h + 1), :], v_ones[p][:, kt, h, :],
                                           probs[:, rt % 2, h, :], start=(kt == 0), stop=(kt == KT - 1),
                                           skip_group_check=True)
                ins.then_inc(pv_done, 1)

            def transpose_max(c):
                pe.wait_ge(mx_split, c + 1)
                pe.wait_ge(mx_copied, c)
                nc.tensor.transpose(mx_t[:, 0:P], mx_parts[:, :], ident_b[:, :]).then_inc(mx_transposed, 1)

            pe.wait_ge(consts_done, 2)
            pe.wait_ge(stack_loaded[0], STACK_LOAD)
            for r in range(LEAD):
                for half in range(2):
                    max_scores(0, r, half)
                if r == MPC + 1:
                    transpose_max(0)
            pe.wait_ge(ones_done, 4)
            pe.wait_ge(shift_loaded, SHIFT_LOAD)
            for h in range(G):
                scores(0, 0, h)

            def phase2(i, last):
                for j in range(STEPS):
                    t = STEPS * i + j
                    if (j + 1) % KT == 0 and not (last and j == STEPS - 1):
                        pe.wait_ge(shift_loaded, SHIFT_LOAD * (4 * i + (j + 1) // KT + 1))
                    r = 2 * j + LEAD
                    ahead = not (last and r >= 2 * MPG)
                    behind = not (last and j == STEPS - 1)
                    if ahead and r % MPG == 0:
                        p = (r // MPG) % 2
                        pe.wait_ge(stack_loaded[p], STACK_LOAD * (i + 1 + (r // MPG) // 2))
                    for h, halves in enumerate((((0, 0),), ((0, 1), (1, 0)), ((1, 1),), ())):
                        if behind:
                            scores(t + 1, j + 1, h)
                        if ahead:
                            for u, half in halves:
                                max_scores(i, r + u, half)
                    if j % KT == 0:
                        pe.wait_ge(pv_free, START + 4 * i + j // KT)
                    if j % (QC * KT) == 0:
                        pe.wait_ge(v_ready, 2 * i + j // (QC * KT) + 1)
                    times_v(t, j)
                    if j % KT == 4 and not (last and j == STEPS - 4):
                        transpose_max(4 * i + j // KT + 1)

            with pe.Fori(0, BODIES - 1) as i:
                phase2(i, False)
            phase2(BODIES - 1, True)

            for k in range(2):
                pe.wait_ge(exp_done[k], GROUPS * QC * EPC // 2)
                pe.wait_ge(mscore_free[k], GROUPS * MPG // 2)
            pe.wait_ge(pv_free, START + GROUPS * QC)
            pe.wait_ge(mx_copied, GROUPS * QC)
            pe.wait_ge(ffn_cast, 3)

            def attn_out(m):
                pe.wait_ge(y_normed, m + 1)
                for t in range(TPC):
                    for k in range(KC):
                        ins = nc.tensor.matmul(ad_ps[:, t * C:(t + 1) * C], y_n[:, k, t * P:(t + 1) * P],
                                               wo_sb[:, k, :], start=(k == 0), stop=(k == KC - 1))
                ins.then_inc(a_done, 1)

            def transpose_x1(m, s):
                pe.wait_ge(x1_ready, m + 1)
                for k in range(KC):
                    for t in range(TPC):
                        ins = nc.tensor.transpose(b_ps[:, k * CH + t * P:k * CH + (t + 1) * P],
                                                  x1[s][:, t, k * P:(k + 1) * P], ident_f[:, :])
                ins.then_inc(b_done, 1)

            def gate_up(n, s, tiles):
                for o in tiles:
                    if o == 0:
                        pe.wait_ge(x1t_ready, n + 1)
                    cols = slice(o * P, (o + 1) * P)
                    for acc, w, freed, full in ((g_ps[o % 2], wg_sb, silu_done[o % 2], g_full),
                                                (u_ps[o % 2], wu_sb, fused_done[o % 2], u_full)):
                        pe.wait_ge(freed, START + OT // 2 * n + o // 2)
                        passes = [(x[s], k) for x in (x1t_hi, x1t_lo) for k in range(KC)]
                        for m, (x, k) in enumerate(passes):
                            ins = nc.tensor.matmul(acc, w[:, k, cols], x[:, k, :],
                                                   start=(m == 0), stop=(m == len(passes) - 1))
                        ins.then_inc(full, 1)

            def down(n, s):
                for k in range(2):
                    pe.wait_ge(f_lo_done[k], START + OT // 2 * (n + 1))
                for t in range(TPC):
                    passes = [(f[s], o) for f in (f_hi, f_lo) for o in range(OT)]
                    for m, (f, o) in enumerate(passes):
                        ins = nc.tensor.matmul(ad_ps[:, t * C:(t + 1) * C], f[:, o, t * P:(t + 1) * P],
                                               wd_sb[:, o, :], start=(m == 0), stop=(m == len(passes) - 1))
                ins.then_inc(d_done, 1)

            attn_out(0)
            transpose_x1(0, 0)
            gate_up(0, 0, (0, 1, 2, 3))
            pe.wait_ge(attn_read, 1)
            attn_out(1)

            def phase3(n, s, left):
                gate_up(n, s, (4, 5, 6))
                if left > 0:
                    transpose_x1(n + 1, 1 - s)
                gate_up(n, s, (7,))
                if left > 0:
                    gate_up(n + 1, 1 - s, (0, 1))
                pe.wait_ge(attn_read, n + 2 if left > 0 else n + 1)
                down(n, s)
                if left > 0:
                    gate_up(n + 1, 1 - s, (2, 3))
                if left > 1:
                    pe.wait_ge(down_read, START + n + 1)
                    attn_out(n + 2)

            with pe.Fori(0, CHUNKS // 2 - 1) as i:
                for s in range(2):
                    phase3(2 * i + s, s, 2)
            for s in range(2):
                phase3(CHUNKS - 2 + s, s, 1 - s)

        @block.scalar
        def _(act):
            def x_high(n, i, s):
                act.wait_ge(x_loaded[s], 16 * (i + 1))
                nc.scalar.activation(x_hi[s][:, :, :], x_raw[:, s, :, :], ACT.Copy).then_inc(x_hi_done, 1)

            x_high(0, 0, 0)
            for n in range(3):
                act.wait_ge(w_loaded[n], 16)
                nc.scalar.activation(w_hi[:, :, w_piece[n]], w_raw[:, :, w_piece[n]], ACT.Copy)\
                  .then_inc(w_hi_done, 1)
            x_high(1, 0, 1)

            def phase1(i, last):
                for s in range(2):
                    n = 2 * i + s
                    for side in range(2):
                        b = 3 * side + 2
                        act.wait_ge(proj_done, 8 * n + b + 1)
                        act.wait_ge(parts_stored[2 * side + 1], START + PARTS_STORE * n)
                        nc.scalar.activation(parts[:, 2 * side + 1, 0, :], bank[b], ACT.Copy)\
                          .then_inc(hi_done[2 * side + 1], 1)
                        act.wait_ge(rope_added[side], START + n + 1)
                        act.wait_ge(parts_stored[2 * side], START + PARTS_STORE * n)
                        nc.scalar.activation(parts[:, 2 * side, 0, :], roped[:, side, :], ACT.Copy)\
                          .then_inc(hi_done[2 * side], 1)
                    for v in range(2):
                        act.wait_ge(proj_done, 8 * n + 7 + v)
                        for t in range(2):
                            ins = nc.scalar.activation(
                                v_all[:, ds(i, 1), :, s * TPC + 2 * v + t, :].rearrange("p a g d -> p (a g) d"),
                                bank[6 + v][:, t * C:(t + 1) * C].rearrange("p (g d) -> p g d", g=GPB), ACT.Copy)
                        ins.then_inc(p1_bank_free[6 + v], 1)
                    if not last:
                        act.wait_ge(proj_done, 8 * n + 8)
                        x_high(n + 2, i + 1, s)

            with act.Fori(0, BATCH - 1) as i:
                phase1(i, False)
            phase1(BATCH - 1, True)

            def exps(t, rt):
                for h in range(G):
                    act.wait_ge(score_full, START + G * t + h + 1)
                    nc.scalar.activation(probs[:, rt % 2, h, :], score[h % 2], ACT.Exp, scale=SCALE)\
                      .then_inc(exp_done[h % 2], 1)

            exps(0, 0)

            def phase2(i, last):
                for j in range(STEPS):
                    t = STEPS * i + j
                    if not (last and j == STEPS - 1):
                        act.wait_ge(pv_done, START + t)
                        exps(t + 1, j + 1)
                    if j % KT == KT - 1:
                        k = j // KT
                        act.wait_ge(pv_done, START + t + 1)
                        act.wait_ge(o_stored[k % 2], START + O_STORE * (2 * i + k // 2))
                        nc.scalar.activation(o_sb[:, k % 2, :], pv, ACT.Copy).then_inc(pv_free, 1)

            with act.Fori(0, BODIES - 1) as i:
                phase2(i, False)
            phase2(BODIES - 1, True)

            def x1t_high(m, s):
                act.wait_ge(b_done, m + 1)
                nc.scalar.activation(x1t_hi[s][:, :, :], b_ps.rearrange("p (k t) -> p k t", k=KC), ACT.Copy)\
                  .then_inc(x1t_hi_done, 1)

            def silu_gate(n, o):
                act.wait_ge(g_full, OT * n + o + 1)
                act.wait_ge(fused_done[o % 2], START + OT // 2 * n + o // 2)
                nc.scalar.activation(silu[:, o % 2, :], g_ps[o % 2], ACT.Silu, scale=sg_sb[:, o:o + 1])\
                  .then_inc(silu_done[o % 2], 1)

            def fused_high(n, s, o):
                act.wait_ge(fused_done[o % 2], START + OT // 2 * n + o // 2 + 1)
                nc.scalar.activation(f_hi[s][:, o, :], fused[:, o % 2, :], ACT.Copy).then_inc(f_hi_done, 1)

            def first_half(n, s):
                silu_gate(n, 0)
                silu_gate(n, 1)
                fused_high(n, s, 0)
                silu_gate(n, 2)
                fused_high(n, s, 1)
                silu_gate(n, 3)
                fused_high(n, s, 2)
                fused_high(n, s, 3)

            act.wait_ge(ffn_loaded, 16 * 7)
            x1t_high(0, 0)
            first_half(0, 0)

            def phase3(n, s, left):
                silu_gate(n, 4)
                silu_gate(n, 5)
                fused_high(n, s, 4)
                silu_gate(n, 6)
                fused_high(n, s, 5)
                if left > 0:
                    x1t_high(n + 1, 1 - s)
                fused_high(n, s, 6)
                silu_gate(n, 7)
                fused_high(n, s, 7)
                if left > 0:
                    act.wait_ge(d_done, START + n)
                    first_half(n + 1, 1 - s)

            with act.Fori(0, CHUNKS // 2 - 1) as i:
                for s in range(2):
                    phase3(2 * i + s, s, 2)
            for s in range(2):
                phase3(CHUNKS - 2 + s, s, 1 - s)

        @block.vector
        def _(dve):
            for n in range(3):
                dve.wait_ge(w_hi_done, n + 1)
                nc.vector.tensor_tensor(w_lo[:, :, w_piece[n]], w_raw[:, :, w_piece[n]],
                                        w_hi[:, :, w_piece[n]].bitcast(fp32), ALU.subtract).then_inc(w_lo_done, 1)
            dve.wait_ge(tables_loaded, 32)

            def phase1(i):
                for s in range(2):
                    n = 2 * i + s
                    cols = slice(s * CH, (s + 1) * CH)

                    def rope(side):
                        b = 3 * side
                        dve.wait_ge(proj_done, 8 * n + b + 2)
                        dve.wait_ge(rope_added[side], START + n)
                        nc.vector.tensor_tensor(rope_a[:, side, :], bank[b], cos_sb[:, cols], ALU.mult)\
                          .then_inc(p1_bank_free[b], 1)
                        nc.vector.tensor_tensor(rope_r[:, side, :], bank[b + 1], sin_sb[:, cols], ALU.mult)\
                          .then_inc(p1_bank_free[b + 1], 1)

                    def take_rest(a):
                        dve.wait_ge(hi_done[a], n + 1)
                        dve.wait_ge(mid_done[a], START + n)
                        side = a // 2
                        src = bank[3 * side + 2] if a % 2 else roped[:, side, :]
                        ins = nc.vector.tensor_tensor(rest[:, a, :], src, parts[:, a, 0, :], ALU.subtract)
                        ins.then_inc(rest_done[a], 1)

                    def low(a):
                        dve.wait_ge(mid_done[a], START + n + 1)
                        nc.vector.tensor_tensor(parts[:, a, 2, :], rest[:, a, :], parts[:, a, 1, :],
                                                ALU.subtract).then_inc(lo_done[a], 1)

                    rope(0)
                    take_rest(1)
                    rope(1)
                    take_rest(0)
                    low(1)
                    take_rest(3)
                    low(0)
                    take_rest(2)
                    low(3)
                    low(2)

            with dve.Fori(0, BATCH) as i:
                phase1(i)

            def row_max(i, r):
                dve.wait_ge(mscore_full, 2 * MPG * i + r + 1)
                nc.vector.tensor_reduce(out=mx[:, (r // MPC) % 2, r % MPC:r % MPC + 1], in_=mscore[r % 2],
                                        axis=AX.X, op=ALU.max).then_inc(mscore_free[r % 2], 1)

            def split_max(c, rc):
                m = mx[:, rc % 2, :]
                for k in range(2):
                    dve.wait_ge(mscore_free[k], MPC // 2 * (c + 1))
                nc.vector.tensor_scalar(mx_part[0], m, -1.0, None, ALU.mult).then_inc(mx_step, 1)
                dve.wait_ge(mx_step, 3 * c + 1)
                nc.vector.scalar_tensor_tensor(out=mx_rest[:, :], in0=m, scalar=-1.0, in1=mx_part[0],
                                               op0=ALU.mult, op1=ALU.subtract).then_inc(mx_step, 1)
                dve.wait_ge(mx_step, 3 * c + 2)
                nc.vector.tensor_copy(mx_part[1], mx_rest[:, :]).then_inc(mx_step, 1)
                dve.wait_ge(mx_step, 3 * c + 3)
                nc.vector.tensor_tensor(mx_part[2], mx_rest[:, :], mx_part[1], ALU.subtract)\
                  .then_inc(mx_split, 1)

            def copy_rows(c):
                dve.wait_ge(mx_transposed, c + 1)
                dve.wait_ge(shift_loaded, SHIFT_LOAD * c)
                nc.vector.tensor_copy(mx_rows[:, :], mx_t[0:PARTS * MPC, 0:P]).then_inc(mx_copied, 1)

            nc.vector.memset(mx_parts[:, PARTS * MPC:P], 0.0)
            for r in range(MPC):
                row_max(0, r)
            split_max(0, 0)
            for r in range(MPC, LEAD):
                row_max(0, r)
            copy_rows(0)

            def invert(b):
                dve.wait_ge(sums_loaded[b // 3], 16 * (3 if b < 3 else 1))
                nc.vector.reciprocal(sums_sb[:, b, :], sums_sb[:, b, :]).then_inc(rinv_done, 1)

            def phase2(i, last):
                for j in range(STEPS):
                    for r in (2 * j + LEAD, 2 * j + LEAD + 1):
                        if not (last and r >= 2 * MPG):
                            row_max(i, r)
                    if not (last and j // KT == STEPS // KT - 1):
                        if j % KT == 3:
                            split_max(4 * i + j // KT + 1, j // KT + 1)
                        if j % KT == 4:
                            copy_rows(4 * i + j // KT + 1)
                    if last and j in (20, 22, 24):
                        invert(j // 2 - 10)

            with dve.Fori(0, BODIES - 1) as i:
                phase2(i, False)
            phase2(BODIES - 1, True)

            def moments(m, k, step, steps, src):
                def stepped(ins, at):
                    ins.then_inc(ln_step[k], 1)
                    dve.wait_ge(ln_step[k], steps * m + step + at)

                for t in range(TPC):
                    ins = nc.vector.bn_stats(st[:, k, t, :], src[:, t, :])
                stepped(ins, 1)
                mean_e, dev_e, mean_o, dev_o = (st[:, k, :, c] for c in (1, 2, 4, 5))
                nc.vector.tensor_tensor(ln_mean[:, k, :], mean_e, mean_o, ALU.add)
                nc.vector.tensor_tensor(ln_diff[:, k, :], mean_e, mean_o, ALU.subtract)
                stepped(nc.vector.tensor_tensor(ln_dev[:, k, :], dev_e, dev_o, ALU.add), 2)
                nc.vector.tensor_scalar(ln_mean[:, k, :], ln_mean[:, k, :], 0.5, None, ALU.mult)
                nc.vector.tensor_scalar(ln_dev[:, k, :], ln_dev[:, k, :], 1.0 / C, EPS, ALU.mult, ALU.add)
                stepped(nc.vector.scalar_tensor_tensor(out=ln_diff[:, k, :], in0=ln_diff[:, k, :], scalar=0.25,
                                                       in1=ln_diff[:, k, :], op0=ALU.mult, op1=ALU.mult), 3)
                nc.vector.tensor_tensor(var_eps[:, k, :], ln_dev[:, k, :], ln_diff[:, k, :], ALU.add)\
                  .then_inc(var_ready[k], 1)

            def normalise(m, k, src, dst, done):
                dve.wait_ge(rstd_ready[k], m + 1)
                for t in range(TPC):
                    ins = nc.vector.tensor_scalar(dst[:, t, :], src[:, t, :], ln_mean[:, k, t:t + 1],
                                                  rstd[:, k, t:t + 1], ALU.subtract, ALU.mult)
                    if k == 1 or t == TPC - 1:
                        ins.then_inc(done, 1)

            def moments1(m):
                dve.wait_ge(a_done, m + 1)
                dve.wait_ge(y_loaded, Y_LOAD * (m + 1))
                nc.vector.tensor_tensor(res1[:, :, :], ad_ps.rearrange("p (t c) -> p t c", c=C), x_in[:, :, :],
                                        ALU.add).then_inc(attn_read, 1)
                dve.wait_ge(attn_read, m + 1)
                moments(m, 0, 0, 3, res1)

            def moments2(m, s):
                dve.wait_ge(d_done, START + m + 1)
                nc.vector.tensor_tensor(res2[:, :, :], ad_ps.rearrange("p (t c) -> p t c", c=C),
                                        sd_sb[:, :].unsqueeze(1).to_broadcast([P, TPC, C]), ALU.mult)\
                  .then_inc(down_read, 1)
                dve.wait_ge(down_read, START + m + 1)
                nc.vector.tensor_tensor(res2[:, :, :], res2[:, :, :], x1[s][:, :, :], ALU.add)\
                  .then_inc(ln_step[1], 1)
                dve.wait_ge(ln_step[1], 4 * m + 1)
                moments(m, 1, 1, 4, res2)

            def fuse(n, o):
                dve.wait_ge(u_full, OT * n + o + 1)
                dve.wait_ge(silu_done[o % 2], START + OT // 2 * n + o // 2 + 1)
                dve.wait_ge(f_lo_done[o % 2], START + OT // 2 * n + o // 2)
                nc.vector.scalar_tensor_tensor(out=fused[:, o % 2, :], in0=u_ps[o % 2], scalar=su_sb[:, o:o + 1],
                                               in1=silu[:, o % 2, :], op0=ALU.mult, op1=ALU.mult)\
                  .then_inc(fused_done[o % 2], 1)

            def x1t_low(m, s):
                dve.wait_ge(x1t_hi_done, m + 1)
                nc.vector.tensor_tensor(x1t_lo[s][:, :, :], b_ps.rearrange("p (k t) -> p k t", k=KC),
                                        x1t_hi[s][:, :, :].bitcast(fp32), ALU.subtract).then_inc(x1t_ready, 1)

            dve.wait_ge(ffn_loaded, 16 * 7)
            moments1(0)
            normalise(0, 0, res1, x1[0], x1_ready)
            x1t_low(0, 0)
            for o in range(OT // 2):
                fuse(0, o)
            invert(3)

            def phase3(n, s, left):
                if left > 0:
                    moments1(n + 1)
                fuse(n, 4)
                if left > 0:
                    normalise(n + 1, 0, res1, x1[1 - s], x1_ready)
                fuse(n, 5)
                fuse(n, 6)
                if left > 0:
                    x1t_low(n + 1, 1 - s)
                fuse(n, 7)
                if left > 0:
                    fuse(n + 1, 0)
                    fuse(n + 1, 1)
                moments2(n, s)
                if left > 0:
                    fuse(n + 1, 2)
                dve.wait_ge(out_stored, START + 16 * n)
                normalise(n, 1, res2, out_sb, out_ready)
                if left > 0:
                    fuse(n + 1, 3)

            with dve.Fori(0, CHUNKS // 2 - 1) as i:
                for s in range(2):
                    phase3(2 * i + s, s, 2)
            for s in range(2):
                phase3(CHUNKS - 2 + s, s, 1 - s)

        @block.gpsimd
        def _(pool):
            for count in from_start:
                pool.sem_inc(count, START)
            nc.gpsimd.memset(ident_f[:, :], 0.0).then_inc(ident0, 1)
            nc.gpsimd.memset(ident_b[:, :], 0.0).then_inc(ident0, 1)
            nc.gpsimd.memset(neg_half[:, :], -0.5).then_inc(ident0, 1)
            pool.wait_ge(ident0, 3)
            nc.gpsimd.affine_select(out=ident_f[:, :], in_=ident_f[:, :], compare_op=ALU.not_equal, fill=1.0,
                                    base=0, pattern=[[-1, P]], channel_multiplier=1).then_inc(consts_done, 1)
            nc.gpsimd.affine_select(out=ident_b[:, :], in_=ident_b[:, :], compare_op=ALU.not_equal, fill=1.0,
                                    base=0, pattern=[[-1, P]], channel_multiplier=1).then_inc(consts_done, 1)

            def x_low(n, s):
                pool.wait_ge(x_hi_done, n + 1)
                nc.gpsimd.tensor_tensor(x_lo[s][:, :, :], x_raw[:, s, :, :], x_hi[s][:, :, :].bitcast(fp32),
                                        ALU.subtract).then_inc(x_lo_done, 1)

            x_low(0, 0)
            x_low(1, 1)

            def phase1(i, last):
                for s in range(2):
                    n = 2 * i + s

                    def add_rope(side):
                        pool.wait_ge(p1_bank_free[3 * side], START + n + 1)
                        pool.wait_ge(p1_bank_free[3 * side + 1], START + n + 1)
                        pool.wait_ge(rest_done[2 * side], START + n)
                        nc.gpsimd.tensor_tensor(roped[:, side, :], rope_a[:, side, :], rope_r[:, side, :],
                                                ALU.add).then_inc(rope_added[side], 1)

                    def middle(a):
                        pool.wait_ge(ident0, 3)
                        pool.wait_ge(rest_done[a], START + n + 1)
                        nc.gpsimd.tensor_copy(parts[:, a, 1, :], rest[:, a, :]).then_inc(mid_done[a], 1)

                    add_rope(0)
                    middle(1)
                    add_rope(1)
                    middle(0)
                    middle(3)
                    middle(2)
                    if not last:
                        x_low(n + 2, s)

            with pool.Fori(0, BATCH - 1) as i:
                phase1(i, False)
            phase1(BATCH - 1, True)

            pool.wait_ge(mid_done[2], START + CHUNKS)
            for n, ones in enumerate((k_stack[0][STACK:SHIFT, :, :], v_ones[0][:, :, :, :],
                                      k_stack[1][STACK:SHIFT, :, :], v_ones[1][:, :, :, :])):
                nc.gpsimd.memset(ones, 1.0).then_inc(ones_done, 1)
                pool.wait_ge(ones_done, n + 1)

            def place_v(g, b, hg, p):
                nc.gpsimd.tensor_copy(
                    v_ones[p][:, :, :, 0:HD],
                    v_all[:, ds(b, 1), ds(hg, 1), :, :].rearrange("p a b k (h d) -> p (a b k) h d", d=HD))\
                  .then_inc(v_ready, 1)

            for v in range(2):
                pool.wait_ge(p1_bank_free[6 + v], START + CHUNKS)
            place_v(0, 0, 0, 0)
            pool.wait_ge(ffn_loaded, 16 * 7)
            for w, n, k in ((wg_sb, 0, KC), (wu_sb, 1, KC), (wd_sb, 2, OT)):
                nc.gpsimd.tensor_copy(w[:, :, :], w8_sb[:, n, :].bitcast(i8).rearrange("p (k o) -> p k o", k=k))\
                  .then_inc(ffn_cast, 1)

            def phase2(i, last):
                g = 2 * i + 1
                pool.wait_ge(ones_done, 4)
                pool.wait_ge(pv_done, START + STEPS * i)
                place_v(g, g // GPB, g % GPB, 1)
                if not last:
                    g = 2 * i + 2
                    pool.wait_ge(ones_done, 4)
                    pool.wait_ge(pv_done, START + STEPS * i + STEPS // 2)
                    place_v(g, g // GPB, g % GPB, 0)

            with pool.Fori(0, BODIES - 1) as i:
                phase2(i, False)
            phase2(BODIES - 1, True)

            pool.wait_ge(ident0, 3)

            def norm_y(m):
                pool.wait_ge(y_loaded, Y_LOAD * (m + 1))
                pool.wait_ge(a_done, m)
                nc.gpsimd.tensor_tensor(y_n[:, :, :], y_in[:, :, :], r_in[:, :, :], ALU.mult).then_inc(y_normed, 1)

            def root(m, k):
                pool.wait_ge(var_ready[k], m + 1)
                nc.gpsimd.tensor_tensor(rstd[:, k, :], var_eps[:, k, :], neg_half[:, :], ALU.pow)\
                  .then_inc(rstd_ready[k], 1)

            def fused_low(n, s, tiles):
                for o in tiles:
                    pool.wait_ge(f_hi_done, OT * n + o + 1)
                    nc.gpsimd.tensor_tensor(f_lo[s][:, o, :], fused[:, o % 2, :],
                                            f_hi[s][:, o, :].bitcast(fp32), ALU.subtract)\
                      .then_inc(f_lo_done[o % 2], 1)

            norm_y(0)
            root(0, 0)
            norm_y(1)
            fused_low(0, 0, (0, 1, 2, 3))

            def phase3(n, s, left):
                if left > 0:
                    root(n + 1, 0)
                fused_low(n, s, (4, 5, 6, 7))
                if left > 1:
                    norm_y(n + 2)
                if left > 0:
                    fused_low(n + 1, 1 - s, (0, 1))
                root(n, 1)
                if left > 0:
                    fused_low(n + 1, 1 - s, (2, 3))

            with pool.Fori(0, CHUNKS // 2 - 1) as i:
                for s in range(2):
                    phase3(2 * i + s, s, 2)
            for s in range(2):
                phase3(CHUNKS - 2 + s, s, 1 - s)


def kernel(**inputs):
    import numpy as np
    import concourse.bacc as bacc
    from concourse import mybir
    from concourse.bass_utils import run_bass_kernel_spmd

    HEADS, HD, HALF, T = 16, 16, 8, 1024
    x = np.asarray(inputs["L0_attn_x"])
    B, _, C = x.shape
    x_nat = np.ascontiguousarray(x.reshape(B * T, C))
    heads = np.arange(HEADS)[:, None] * HD
    d = np.arange(HALF)[None, :]
    rotary = (heads + d).ravel()
    partner = (heads + (d + HALF // 2) % HALF).ravel()
    plain = (heads + HALF + d).ravel()
    wq, wk, wv, wo = (np.asarray(inputs[f"L0_attn_{n}"]) for n in ("wq", "wk", "wv", "wo"))
    w_qkv = np.ascontiguousarray(np.concatenate(
        [wq.T[:, rotary], wq.T[:, partner], wq.T[:, plain],
         wk.T[:, rotary], wk.T[:, partner], wk.T[:, plain], wv.T], axis=1))
    inv_freq = (1.0 / np.float32(10000.0) ** (np.arange(0, HD, 2, dtype=np.float32) / np.float32(HD))).astype(np.float32)
    angle = inv_freq[:, None] * np.arange(T, dtype=np.float32)[None, :]
    sign = np.where(np.arange(HALF) < HALF // 2, -1.0, 1.0).astype(np.float32)[:, None]
    cos = np.tile(np.cos(angle), (HEADS, 1)).astype(np.float32)
    sin = np.tile(sign * np.sin(angle), (HEADS, 1)).astype(np.float32)
    arrays = {
        "x_nat": x_nat,
        "x_cols": np.ascontiguousarray(x_nat.T),
        "w_qkv": w_qkv,
        "w_out": np.ascontiguousarray(wo.T),
        "rope_cos": cos,
        "rope_sin": sin,
    }
    for name in ("w_gate", "w_up", "w_down", "s_gate", "s_up", "s_down"):
        arrays[name] = np.ascontiguousarray(np.asarray(inputs[f"L0_ffn_{name}"]))
    for name in ("w_gate", "w_up", "w_down"):
        arrays[name] = arrays[name].view(np.int32)
    for name in ("s_gate", "s_up"):
        arrays[name] = np.ascontiguousarray(arrays[name].reshape(-1, 128).T)
    nc = bacc.Bacc("TRN2", target_bir_lowering=False, num_devices=1)
    args = [nc.dram_tensor(n, a.shape, mybir.dt.from_np(a.dtype), kind="ExternalInput").ap()
            for n, a in arrays.items()]
    out = nc.dram_tensor("out", (B * T, C), mybir.dt.float32, kind="ExternalOutput").ap()
    build_attention_ffn_block(nc, *args, out)
    r = run_bass_kernel_spmd(nc, [arrays], core_ids=[0])
    return r.results[0]["out"].reshape(B, T, C)
```

```python
import concourse.bass as bass
from concourse import mybir
from contextlib import ExitStack


def build_attention_ffn_block(nc, x_nat, x_cols, w_qkv, w_out, rope_cos, rope_sin,
                              w_gate, w_up, w_down, s_gate, s_up, s_down, out):
    fp32, fp32r, bf16, i8 = mybir.dt.float32, mybir.dt.float32r, mybir.dt.bfloat16, mybir.dt.int8
    ALU, ACT, AX = mybir.AluOpType, mybir.ActivationFunctionType, mybir.AxisListType
    ds = bass.ds

    P = 128
    TOKENS, C = x_nat.shape
    BATCH = 4
    T = TOKENS // BATCH
    NH, HD = 16, 16
    HALF = HD // 2
    INTER = 4 * w_gate.shape[1]
    KC = C // P
    NB = 512
    CH = NB
    CHUNKS = TOKENS // CH
    TPC = CH // P
    G = 4
    GROUPS = BATCH * NH // G
    GPB = NH // G
    KT = T // P
    QC = T // CH
    PARTS = 3
    TERMS_Q, TERMS_K = (0, 0, 1, 0, 2, 1), (0, 1, 0, 2, 0, 1)
    NT = len(TERMS_Q)
    STACK = NT * HD
    SHIFT = STACK + PARTS
    SCALE = float(HD) ** -0.5
    OT = INTER // P
    EPS = 1e-5

    STEPS = 4 * KT
    BODIES = GROUPS // 2
    LEAD = 24
    MPC = G * TPC
    MPG = QC * MPC
    EPC = KT * G
    FIRST_T = MPC + 3

    INVERT_STEPS = (4, 5, 6)
    Y0_STEP = 20
    ATTN0_STEP, X1T0_STEP = 22, 28

    q_parts = nc.dram_tensor("q_parts", [BATCH * C, PARTS, T], bf16).ap()
    k_parts = nc.dram_tensor("k_parts", [BATCH * C, PARTS, T], bf16).ap()
    y_raw = nc.dram_tensor("y_raw", [BATCH * C, T], fp32).ap()
    row_sums = nc.dram_tensor("row_sums", [BATCH * NH, T], fp32).ap()
    row_rinv = nc.dram_tensor("row_rinv", [BATCH * NH, T], fp32).ap()

    ctx = ExitStack()
    with ctx:
        def sb_in(stack, name, shape, dt):
            return stack.enter_context(nc.sbuf_tensor(name, shape, dt))

        def sb(name, shape, dt):
            return sb_in(ctx, name, shape, dt)

        def sem(name):
            return ctx.enter_context(nc.semaphore(name))

        v_all = sb("v_all", [P, BATCH, GPB, KT, G * HD], fp32)
        wo_sb = sb("wo_sb", [P, KC, C], fp32)
        wo_hi = sb("wo_hi", [P, KC, C], fp32r)
        wo_lo = sb("wo_lo", [P, KC, C], fp32r)
        wg_sb = sb("wg_sb", [P, KC, INTER], fp32r)
        wu_sb = sb("wu_sb", [P, KC, INTER], fp32r)
        wd_sb = sb("wd_sb", [P, OT, C], fp32r)
        sg_sb = sb("sg_sb", [P, OT], fp32)
        su_sb = sb("su_sb", [P, OT], fp32)
        sd_sb = sb("sd_sb", [P, C], fp32)
        neg_half = sb("neg_half", [P, TPC], fp32)
        ident_f = sb("ident_f", [P, P], fp32)
        ident_b = sb("ident_b", [P, P], bf16)

        with ExitStack() as late:
            f_hi = [sb_in(late, f"f_hi{s}", [P, OT, CH], fp32r) for s in range(2)]
            f_lo = [sb_in(late, f"f_lo{s}", [P, OT, CH], fp32r) for s in range(2)]

        q_stack = [sb(f"q_stack{p}", [SHIFT, QC, G, CH], bf16) for p in range(2)]
        k_stack = [sb(f"k_stack{p}", [SHIFT, G, T], bf16) for p in range(2)]
        v_ones = [sb(f"v_ones{p}", [P, KT, G, 2 * HD], fp32) for p in range(2)]
        with ExitStack() as raw:
            w_raw = sb_in(raw, "w_raw", [P, KC, 8 * P], fp32)
            x_raw = sb_in(raw, "x_raw", [P, 2, KC, CH], fp32)
        probs = sb("probs", [P, 2, G, CH], fp32)
        mx = sb("mx", [P, 2, MPC], fp32)
        mx_rest = sb("mx_rest", [P, MPC], fp32)
        mx_parts = sb("mx_parts", [P, P], bf16)
        mx_rows = sb("mx_rows", [PARTS * MPC, P], bf16)
        o_sb = sb("o_sb", [P, 2, CH], fp32)
        w8_sb = sb("w8_sb", [P, 3, KC * INTER // 4], mybir.dt.int32)

        with ExitStack() as p1:
            w_hi = sb_in(p1, "w_hi", [P, KC, 8 * P], fp32r)
            w_lo = sb_in(p1, "w_lo", [P, KC, 8 * P], fp32r)
            cos_sb = sb_in(p1, "cos_sb", [P, T], fp32)
            sin_sb = sb_in(p1, "sin_sb", [P, T], fp32)
            x_hi = [sb_in(p1, f"x_hi{s}", [P, KC, CH], fp32r) for s in range(2)]
            x_lo = [sb_in(p1, f"x_lo{s}", [P, KC, CH], fp32r) for s in range(2)]
            rope_a = sb_in(p1, "rope_a", [P, 2, CH], fp32)
            rope_r = sb_in(p1, "rope_r", [P, 2, CH], fp32)
            roped = sb_in(p1, "roped", [P, 2, CH], fp32)
            rest = sb_in(p1, "rest", [P, 4, CH], fp32)
            parts = sb_in(p1, "parts", [P, 4, PARTS, CH], bf16)

        sums_sb = sb("sums_sb", [P, BATCH, NH * T // P], fp32)
        y_in = sb("y_in", [P, KC, CH], fp32)
        r_in = sb("r_in", [P, KC, CH], fp32)
        x_in = sb("x_in", [P, TPC, C], fp32)
        y_n = sb("y_n", [P, KC, CH], fp32)
        y_hi = sb("y_hi", [P, KC, CH], fp32r)
        y_lo = sb("y_lo", [P, KC, CH], fp32r)
        res1 = sb("res1", [P, TPC, C], fp32)
        x1 = [sb(f"x1_{s}", [P, TPC, C], fp32) for s in range(2)]
        x1t_hi = [sb(f"x1t_hi{s}", [P, KC, CH], fp32r) for s in range(2)]
        x1t_lo = [sb(f"x1t_lo{s}", [P, KC, CH], fp32r) for s in range(2)]
        silu = sb("silu", [P, 2, CH], fp32)
        fused = sb("fused", [P, 2, CH], fp32)
        res2 = sb("res2", [P, TPC, C], fp32)
        out_sb = sb("out_sb", [P, TPC, C], fp32)
        st = sb("st", [P, 2, TPC, 6], fp32)
        ln_mean = sb("ln_mean", [P, 2, TPC], fp32)
        ln_diff = sb("ln_diff", [P, 2, TPC], fp32)
        ln_dev = sb("ln_dev", [P, 2, TPC], fp32)
        var_eps = sb("var_eps", [P, 2, TPC], fp32)
        rstd = sb("rstd", [P, 2, TPC], fp32)

        ps = ctx.enter_context(nc.psum_tensor("ps", [P, 8 * NB], fp32))
        bank = [ps[:, b * NB:(b + 1) * NB] for b in range(8)]
        score = bank[0:2]
        mscore = [ps[:, 4 * NB:6 * NB], ps[:, 6 * NB:8 * NB]]
        ROOMY = range(ATTN0_STEP, X1T0_STEP + 1)

        def score_bank(rt, h, last):
            return bank[(0, 1, 6, 7)[h]] if last and rt in ROOMY else score[h % 2]

        pv = bank[2:4]
        p1_bank = [bank[b % 4] for b in range(8)]
        first_mx_t = bank[4 + 2 * ((FIRST_T + 1) % 2)].bitcast(bf16)
        mx_part = [mx_parts[:, k * MPC:(k + 1) * MPC] for k in range(PARTS)]
        down_ps = ps[:, 0:2 * NB]
        attn_ps = ps[:, 2 * NB:4 * NB]
        attn0_ps, x1t0_ps = mscore[0], mscore[1]
        g_ps, u_ps = [bank[4], bank[6]], [bank[5], bank[7]]

        w_loaded = [sem(f"w_loaded{n}") for n in range(3)]
        tables_loaded, ffn_loaded = sem("tables_loaded"), sem("ffn_loaded")
        x_loaded = [sem(f"x_loaded{s}") for s in range(2)]
        w_hi_done, w_lo_done = sem("w_hi_done"), sem("w_lo_done")
        x_hi_done, x_lo_done = sem("x_hi_done"), sem("x_lo_done")
        proj_done = sem("proj_done")
        proj_read = [sem(f"proj_read{b}") for b in range(8)]
        rope_added = [sem(f"rope_added{s}") for s in range(2)]
        hi_done = [sem(f"hi_done{a}") for a in range(4)]
        rest_done = [sem(f"rest_done{a}") for a in range(4)]
        mid_done = [sem(f"mid_done{a}") for a in range(4)]
        lo_done = [sem(f"lo_done{a}") for a in range(4)]
        proj_read[2], proj_read[6] = rest_done[1], rest_done[3]
        v_copied = [proj_read[3], proj_read[7]]
        parts_stored = [sem(f"parts_stored{a}") for a in range(4)]

        consts_done, ident0 = sem("consts_done"), sem("ident0")
        k_loaded = [sem(f"k_loaded{p}") for p in range(2)]
        q_loaded = [[sem(f"q_loaded{p}_{qc}") for qc in range(QC)] for p in range(2)]
        ones_done = sem("ones_done")
        v_ready = sem("v_ready")
        mscore_full = sem("mscore_full")
        mscore_free = [sem(f"mscore_free{k}") for k in range(2)]
        mx_step, mx_split, mx_transposed = sem("mx_step"), sem("mx_split"), sem("mx_transposed")
        mx_copied, shift_loaded = sem("mx_copied"), sem("shift_loaded")
        score_full = sem("score_full")
        exp_done = [sem(f"exp_done{k}") for k in range(2)]
        pv_done, pv_free = sem("pv_done"), sem("pv_free")
        o_stored = [sem(f"o_stored{p}") for p in range(2)]

        sums_loaded = [sem(f"sums_loaded{k}") for k in range(2)]
        rinv_stored = [sem(f"rinv_stored{k}") for k in range(2)]
        rinv_done = sem("rinv_done")
        y_loaded, x_in_loaded, y_normed = sem("y_loaded"), sem("x_in_loaded"), sem("y_normed")
        y_hi_done, y_lo_done, wo_split = sem("y_hi_done"), sem("y_lo_done"), sem("wo_split")
        a_done, attn_read = sem("a_done"), sem("attn_read")
        ln_step = [sem(f"ln_step{k}") for k in range(2)]
        var_ready = [sem(f"var_ready{k}") for k in range(2)]
        rstd_ready = [sem(f"rstd_ready{k}") for k in range(2)]
        x1_ready = sem("x1_ready")
        b_done, x1t_hi_done, x1t_ready = sem("b_done"), sem("x1t_hi_done"), sem("x1t_ready")
        ffn_cast = sem("ffn_cast")
        g_full, u_full = sem("g_full"), sem("u_full")
        silu_done = [sem(f"silu_done{k}") for k in range(2)]
        fused_done = [sem(f"fused_done{k}") for k in range(2)]
        f_hi_done = sem("f_hi_done")
        f_lo_done = [sem(f"f_lo_done{k}") for k in range(2)]
        d_done, down_read = sem("d_done"), sem("down_read")
        out_ready, out_stored = sem("out_ready"), sem("out_stored")

        START = 1
        from_start = [*proj_read[:2], *proj_read[4:6], *v_copied, *rest_done, *lo_done, *rope_added,
                      *parts_stored, score_full, pv_done, pv_free, *o_stored, *silu_done, *fused_done,
                      *f_lo_done, d_done, down_read, out_ready, out_stored]

        PARTS_STORE = 16
        STACK_LOAD = 16 * NT
        SHIFT_LOAD = 16
        O_STORE = 16 * (G + 1)
        Y_LOAD = 16 * (KC + KC)

        w_piece = [slice(0, 3 * P), slice(6 * P, 8 * P), slice(3 * P, 6 * P)]
        block = ctx.enter_context(nc.Block())

        @block.sync
        def _(sp):
            def load_x(n, s):
                sp.dma_start(x_raw[:, s, :, :],
                             x_cols.rearrange("(k p) t -> p k t", p=P)[:, :, ds(n * CH, CH)])\
                  .then_inc(x_loaded[s], 16)

            def load_w(n):
                sp.dma_start(w_raw[:, :, w_piece[n]], w_qkv.rearrange("(k p) n -> p k n", p=P)[:, :, w_piece[n]])\
                  .then_inc(w_loaded[n], 16)

            load_x(0, 0)
            load_w(0)
            sp.dma_start(cos_sb[:, :], rope_cos).then_inc(tables_loaded, 16)
            sp.dma_start(sin_sb[:, :], rope_sin).then_inc(tables_loaded, 16)
            load_w(1)
            load_w(2)
            load_x(1, 1)
            for n, w in enumerate((w_gate, w_up)):
                sp.dma_start(w8_sb[:, n, :].rearrange("p (k o) -> p k o", k=KC),
                             w.rearrange("(k p) o -> p k o", p=P)).then_inc(ffn_loaded, 16)
            sp.dma_start(w8_sb[:, 2, :].rearrange("p (k o) -> p k o", k=OT),
                         w_down.rearrange("(k p) o -> p k o", p=P)).then_inc(ffn_loaded, 16)
            sp.dma_start(wo_sb[:, :, :], w_out.rearrange("(k p) o -> p k o", p=P)).then_inc(ffn_loaded, 16)
            sp.dma_start(sg_sb[:, :], s_gate).then_inc(ffn_loaded, 16)
            sp.dma_start(su_sb[:, :], s_up).then_inc(ffn_loaded, 16)
            sp.dma_start(sd_sb[:, :], s_down.unsqueeze(0).to_broadcast([P, C])).then_inc(ffn_loaded, 16)

            def load_k(g, p, terms=range(NT)):
                k_rows = k_parts[ds(g * G * HD, G * HD), :, :].rearrange("(h d) part t -> d part h t", d=HD)
                for n in terms:
                    sp.dma_start(k_stack[p][n * HD:(n + 1) * HD, :, :], k_rows[:, TERMS_K[n], :, :])\
                      .then_inc(k_loaded[p], 16)

            def load_q(g, p, qc, terms=range(NT)):
                q_rows = q_parts[ds(g * G * HD, G * HD), :, qc * CH:(qc + 1) * CH]\
                    .rearrange("(h d) part t -> d part h t", d=HD)
                for n in terms:
                    sp.dma_start(q_stack[p][n * HD:(n + 1) * HD, qc, :, :], q_rows[:, TERMS_Q[n], :, :])\
                      .then_inc(q_loaded[p][qc], 16)

            def load_shift(c, rc):
                p, qc = (rc // QC) % 2, rc % QC
                sp.wait_ge(mx_copied, c + 1)
                sp.dma_start(q_stack[p][STACK:SHIFT, qc, :, :].rearrange("a h q -> a (h q)"), mx_rows[:, :])\
                  .then_inc(shift_loaded, 16)

            def phase1(i, last, load_first=False):
                for s in range(2):
                    n = 2 * i + s
                    if not last:
                        sp.wait_ge(x_loaded[0], 16)
                        sp.wait_ge(x_lo_done, n + 1)
                        load_x(n + 2, s)
                    if load_first:
                        if s == 0:
                            load_k(0, 0)
                        load_q(0, 0, s)
                    for a in (1, 0, 3, 2):
                        if last and s == 1 and a == 0:
                            load_shift(0, 0)
                        dst = (q_parts if a < 2 else k_parts)
                        rows = dst[ds(i * C, C), :, s * CH:(s + 1) * CH]\
                            .rearrange("(m j) part t -> j m part t", j=2)[a % 2]
                        sp.wait_ge(x_loaded[0], 16)
                        sp.wait_ge(lo_done[a], START + n + 1)
                        sp.dma_start(rows, parts[:, a, :, :]).then_inc(parts_stored[a], 16)

            with sp.Fori(0, BATCH - 2) as i:
                phase1(i, False)
            for a in range(4):
                sp.wait_ge(parts_stored[a], START + PARTS_STORE * QC)
            phase1(BATCH - 2, False, True)
            phase1(BATCH - 1, True)

            def store_o(i, k):
                c, p, qc = 4 * i + k, k % 2, k % QC
                g = 2 * i + k // QC
                sp.wait_ge(x_loaded[0], 16)
                sp.wait_ge(pv_free, START + c + 1)
                for h in range(G):
                    sp.dma_start(y_raw[ds(g * G * HD + h * HD, HD), qc * CH:(qc + 1) * CH],
                                 o_sb[2 * HD * h:2 * HD * h + HD, p, :]).then_inc(o_stored[p], 16)
                sp.dma_start(row_sums[ds(g * G, G), qc * CH:(qc + 1) * CH],
                             o_sb[HD:P:2 * HD, p, :]).then_inc(o_stored[p], 16)

            load_q(1, 1, 0)
            for a in range(4):
                sp.wait_ge(parts_stored[a], START + PARTS_STORE * CHUNKS)

            def load_sums(batches):
                for b in batches:
                    sp.dma_start(sums_sb[:, b, :], row_sums[b * NH:(b + 1) * NH, :]
                                 .rearrange("r (a t) -> (r a) t", a=P // NH)).then_inc(sums_loaded[b // 3], 16)

            def store_rinv(batches):
                sp.wait_ge(rinv_done, batches[-1] + 1)
                for b in batches:
                    sp.dma_start(row_rinv[b * NH:(b + 1) * NH, :].rearrange("r (a t) -> (r a) t", a=P // NH),
                                 sums_sb[:, b, :]).then_inc(rinv_stored[b // 3], 16)

            def load_y(n):
                b, cols = n // 2, (n % 2) * CH
                for k in range(KC):
                    sp.dma_start(y_in[:, k, :], y_raw[ds(b * C + k * P, P), ds(cols, CH)])\
                      .then_inc(y_loaded, 16)
                    sp.dma_start(r_in[:, k, :],
                                 row_rinv[ds(b * NH + k * (P // HD), P // HD), ds(cols, CH)]
                                 .unsqueeze(1).to_broadcast([P // HD, HD, CH]))\
                      .then_inc(y_loaded, 16)

            def load_x_in(n):
                sp.dma_start(x_in[:, :, :],
                             x_nat[ds(n * CH, CH), :].rearrange("(t p) c -> p t c", p=P))\
                  .then_inc(x_in_loaded, 16)

            def load_next(m):
                sp.wait_ge(x_loaded[0], 16)
                sp.wait_ge(y_normed, m)
                load_y(m)
                sp.wait_ge(x_loaded[0], 16)
                sp.wait_ge(attn_read, m)
                load_x_in(m)

            def phase2(i, last):
                sp.wait_ge(x_loaded[0], 16)
                sp.wait_ge(score_full, START + 2 * QC * EPC * i)
                load_k(2 * i + 1, 1)
                load_q(2 * i + 1, 1, 1)
                if last:
                    for p in range(2):
                        sp.wait_ge(o_stored[p], START + O_STORE * 3 * GPB)
                    load_sums(range(3))
                load_shift(4 * i + 1, 1)
                if last:
                    store_rinv(range(3))
                if not last:
                    sp.wait_ge(x_loaded[0], 16)
                    sp.wait_ge(score_full, START + 2 * QC * EPC * i + EPC)
                    load_q(2 * i + 2, 0, 0)
                store_o(i, 0)
                if last:
                    sp.wait_ge(rinv_stored[0], 16 * 3)
                    load_y(0)
                    load_x_in(0)
                load_shift(4 * i + 2, 2)
                if not last:
                    sp.wait_ge(x_loaded[0], 16)
                    sp.wait_ge(score_full, START + 2 * QC * EPC * i + QC * EPC)
                    load_k(2 * i + 2, 0)
                    load_q(2 * i + 2, 0, 1)
                store_o(i, 1)
                load_shift(4 * i + 3, 3)
                store_o(i, 2)
                if not last:
                    sp.wait_ge(x_loaded[0], 16)
                    sp.wait_ge(score_full, START + 2 * QC * EPC * i + (QC + 1) * EPC)
                    load_q(2 * i + 3, 1, 0)
                    load_shift(4 * i + 4, 4)
                else:
                    load_next(1)
                store_o(i, 3)

            with sp.Fori(0, BODIES - 1) as i:
                phase2(i, False)
            phase2(BODIES - 1, True)

            for p in range(2):
                sp.wait_ge(o_stored[p], START + O_STORE * GROUPS)
            load_sums([BATCH - 1])
            load_next(2)
            store_rinv([BATCH - 1])
            sp.wait_ge(rinv_stored[1], 16)
            with sp.Fori(0, CHUNKS - 3) as n:
                load_next(n + 3)

        @block.tensor
        def _(pe):
            def max_scores(i, r, half):
                p, rg = (r // MPG) % 2, r % MPG
                qc, h, qt = rg // MPC, (rg % MPC) // TPC, rg % TPC
                if half == 0:
                    pe.wait_ge(mscore_free[r % 2], MPG * i + r // 2)
                ins = nc.tensor.matmul(mscore[r % 2][:, half * NB:(half + 1) * NB],
                                       q_stack[p][0:STACK, qc, h, qt * P:(qt + 1) * P],
                                       k_stack[p][0:STACK, h, half * NB:(half + 1) * NB],
                                       start=True, stop=True)
                if half == 1:
                    ins.then_inc(mscore_full, 1)

            def transpose_max(c, dst):
                pe.wait_ge(mx_split, c + 1)
                pe.wait_ge(mx_copied, c)
                nc.tensor.transpose(dst[:, 0:P], mx_parts[:, :], ident_b[:, :]).then_inc(mx_transposed, 1)

            def first_maxima(r):
                if r == 0:
                    pe.wait_ge(k_loaded[0], STACK_LOAD)
                if r % MPC == 0:
                    pe.wait_ge(q_loaded[0][r // MPC], STACK_LOAD)
                if r == FIRST_T + 1:
                    pe.wait_ge(mscore_free[r % 2], r // 2)
                    transpose_max(0, first_mx_t)
                    pe.wait_ge(mx_copied, 1)
                for half in range(2):
                    max_scores(0, r, half)

            def scores(t, rt, h, last=False):
                p, qc, kt = (rt // (QC * KT)) % 2, (rt // KT) % QC, rt % KT
                if last and rt == ROOMY[0] and h >= 2:
                    pe.wait_ge(mscore_free[1], GROUPS * MPG // 2)
                elif last and rt in ROOMY[1:]:
                    pe.wait_ge(exp_done[h % 2], 2 * t + h // 2 - 1)
                else:
                    pe.wait_ge(exp_done[h % 2], 2 * t + h // 2)
                nc.tensor.matmul(score_bank(rt, h, last), k_stack[p][0:SHIFT, h, kt * P:(kt + 1) * P],
                                 q_stack[p][0:SHIFT, qc, h, :],
                                 start=True, stop=True).then_inc(score_full, 1)

            def first_scores(h):
                if h < 2:
                    pe.wait_ge(proj_read[4 + h], START + CHUNKS)
                scores(0, 0, h)

            def phase1(i, maxima=(None, None)):
                for s in range(2):
                    n = 2 * i + s
                    first = maxima[s]
                    pe.wait_ge(w_hi_done, 1)
                    pe.wait_ge(x_hi_done, n + 1)
                    for b in range(8):
                        if b in (3, 4):
                            pe.wait_ge(w_lo_done, (0, 3, 4).index(b) + 1)
                        if b < 4:
                            pe.wait_ge(proj_read[b + 4], START + n)
                        else:
                            pe.wait_ge(proj_read[b - 4], START + n + 1)
                        w_x = ((w_hi, x_hi[s]), (w_hi, x_lo[s]), (w_lo, x_hi[s]))
                        passes = [(w, x, k) for w, x in w_x for k in range(KC)]
                        if b % 4 < 3:
                            cols = slice((3 * (b // 4) + b % 4) * P, (3 * (b // 4) + b % 4 + 1) * P)
                            for m, (w, x, k) in enumerate(passes):
                                if b == 0 and m == KC:
                                    pe.wait_ge(x_lo_done, n + 1)
                                if b == 0 and m == 2 * KC:
                                    pe.wait_ge(w_lo_done, 1)
                                ins = nc.tensor.matmul(p1_bank[b], w[:, k, cols], x[:, k, :],
                                                       start=(m == 0), stop=(m == len(passes) - 1))
                        else:
                            for t in range(2):
                                tile = slice((2 * (b // 4) + t) * P, (2 * (b // 4) + t + 1) * P)
                                for m, (w, x, k) in enumerate(passes):
                                    ins = nc.tensor.matmul(p1_bank[b][:, t * C:(t + 1) * C], x[:, k, tile],
                                                           w[:, k, 6 * P:8 * P],
                                                           start=(m == 0), stop=(m == len(passes) - 1))
                        ins.then_inc(proj_done, 1)
                        if first is not None and first + b == LEAD - 1:
                            pe.wait_ge(ones_done, 2)
                            pe.wait_ge(shift_loaded, SHIFT_LOAD)
                            first_scores(0)
                            first_scores(1)
                        if first is not None:
                            first_maxima(first + b)

            with pe.Fori(0, BATCH - 2) as i:
                phase1(i)
            pe.wait_ge(consts_done, 2)
            phase1(BATCH - 2, (None, 0))
            phase1(BATCH - 1, (LEAD // 3, 2 * LEAD // 3))

            def times_v(t, rt):
                p, kt = (rt // (QC * KT)) % 2, rt % KT
                for k in range(2):
                    pe.wait_ge(exp_done[k], 2 * (t + 1))
                for h in range(G):
                    ins = nc.tensor.matmul(pv[rt // KT % 2][2 * HD * h:2 * HD * (h + 1), :], v_ones[p][:, kt, h, :],
                                           probs[:, rt % 2, h, :], start=(kt == 0), stop=(kt == KT - 1),
                                           skip_group_check=True)
                ins.then_inc(pv_done, 1)

            first_scores(2)
            first_scores(3)
            for b in (6, 7):
                pe.wait_ge(proj_read[b], START + CHUNKS)

            def attn_out(m, dst):
                pe.wait_ge(y_lo_done, m + 1)
                passes = [(y, w, k) for y, w in ((y_hi, wo_hi), (y_hi, wo_lo), (y_lo, wo_hi)) for k in range(KC)]
                for t in range(TPC):
                    for n, (y, w, k) in enumerate(passes):
                        ins = nc.tensor.matmul(dst[:, t * C:(t + 1) * C], y[:, k, t * P:(t + 1) * P],
                                               w[:, k, :], start=(n == 0), stop=(n == len(passes) - 1))
                ins.then_inc(a_done, 1)

            def transpose_x1(m, s, dst):
                pe.wait_ge(x1_ready, m + 1)
                for k in range(KC):
                    for t in range(TPC):
                        ins = nc.tensor.transpose(dst[:, k * CH + t * P:k * CH + (t + 1) * P],
                                                  x1[s][:, t, k * P:(k + 1) * P], ident_f[:, :])
                ins.then_inc(b_done, 1)

            def phase2(i, last):
                for j in range(STEPS):
                    t = STEPS * i + j
                    if (j + 1) == QC * KT:
                        pe.wait_ge(ones_done, 4)
                    if (j + 1) % KT == 0 and not (last and j == STEPS - 1):
                        pe.wait_ge(shift_loaded, SHIFT_LOAD * (4 * i + (j + 1) // KT + 1))
                    r = 2 * j + LEAD
                    ahead = not (last and r >= 2 * MPG)
                    behind = not (last and j == STEPS - 1)
                    if ahead and r % MPC == 0:
                        p, qc = (r // MPG) % 2, (r // MPC) % QC
                        if qc == 0:
                            pe.wait_ge(k_loaded[p], STACK_LOAD * (i + 1 + (r // MPG) // 2))
                        pe.wait_ge(q_loaded[p][qc], STACK_LOAD * (i + 1 + (r // MPG) // 2))
                    for h, halves in enumerate((((0, 0),), ((0, 1), (1, 0)), ((1, 1),), ())):
                        if behind:
                            scores(t + 1, j + 1, h, last)
                        if ahead:
                            for u, half in halves:
                                max_scores(i, r + u, half)
                        if h == 3 and j % KT == 5 and not (last and j == STEPS - 3):
                            c = 4 * i + j // KT + 1
                            pe.wait_ge(pv_free, START + c - 1)
                            transpose_max(c, pv[(j // KT + 1) % 2].bitcast(bf16))
                    if j % KT == 0:
                        pe.wait_ge(mx_copied, 4 * i + j // KT + 1)
                    if j % (QC * KT) == 0:
                        pe.wait_ge(v_ready, 2 * i + j // (QC * KT) + 1)
                    times_v(t, j)
                    if last and j == ATTN0_STEP:
                        for k in range(2):
                            pe.wait_ge(mscore_free[k], GROUPS * MPG // 2)
                        pe.wait_ge(wo_split, 2)
                        attn_out(0, attn0_ps)
                    if last and j == X1T0_STEP:
                        transpose_x1(0, 0, x1t0_ps)

            with pe.Fori(0, BODIES - 1) as i:
                phase2(i, False)
            phase2(BODIES - 1, True)

            pe.wait_ge(ffn_cast, 3)
            pe.wait_ge(ffn_loaded, 16 * 7)

            def gate_up(n, s, o):
                cols = slice(o * P, (o + 1) * P)
                free = START + OT // 2 * n + o // 2

                def product(acc, w, high):
                    x = x1t_hi[s] if high else x1t_lo[s]
                    for k in range(KC):
                        ins = nc.tensor.matmul(acc, w[:, k, cols], x[:, k, :],
                                               start=(high and k == 0), stop=(not high and k == KC - 1))
                    return ins

                if o == 0:
                    pe.wait_ge(x1t_hi_done, n + 1)
                    pe.wait_ge(silu_done[o % 2], free)
                    product(g_ps[0], wg_sb, True)
                    pe.wait_ge(fused_done[o % 2], free)
                    product(u_ps[0], wu_sb, True)
                    pe.wait_ge(x1t_ready, n + 1)
                    product(g_ps[0], wg_sb, False).then_inc(g_full, 1)
                    product(u_ps[0], wu_sb, False).then_inc(u_full, 1)
                else:
                    pe.wait_ge(silu_done[o % 2], free)
                    product(g_ps[o % 2], wg_sb, True)
                    product(g_ps[o % 2], wg_sb, False).then_inc(g_full, 1)
                    pe.wait_ge(fused_done[o % 2], free)
                    product(u_ps[o % 2], wu_sb, True)
                    product(u_ps[o % 2], wu_sb, False).then_inc(u_full, 1)

            def down(n, s, t):
                passes = [(f_hi[s], o) for o in range(OT)] + [(f_lo[s], o) for o in range(OT)]
                if t == 0:
                    pe.wait_ge(down_read, START + n)
                    pe.wait_ge(f_hi_done, OT * (n + 1) - 1)
                    for k in range(2):
                        pe.wait_ge(f_lo_done[k], START + OT // 2 * (n + 1) - 1)
                    passes = ([(f_hi[s], o) for o in range(OT - 1)] + [(f_lo[s], o) for o in range(OT - 2)]
                              + [(f_hi[s], OT - 1), (f_lo[s], OT - 2), (f_lo[s], OT - 1)])
                for m, (f, o) in enumerate(passes):
                    if t == 0 and m == 2 * OT - 3:
                        pe.wait_ge(f_hi_done, OT * (n + 1))
                    if t == 0 and m == 2 * OT - 2:
                        for k in range(2):
                            pe.wait_ge(f_lo_done[k], START + OT // 2 * (n + 1))
                    ins = nc.tensor.matmul(down_ps[:, t * C:(t + 1) * C], f[:, o, t * P:(t + 1) * P],
                                           wd_sb[:, o, :], start=(m == 0), stop=(m == 2 * OT - 1))
                if t % 2 == 1:
                    ins.then_inc(d_done, 1)

            gate_up(0, 0, 0)
            gate_up(0, 0, 1)

            def phase3(n, s, left, first=False):
                if not first:
                    down(n, s, 0)
                if left > 0:
                    gate_up(n + 1, 1 - s, 2)
                if not first:
                    down(n, s, 1)
                if left > 0:
                    gate_up(n + 1, 1 - s, 3)
                if left > 1:
                    attn_out(n + 2, attn_ps)
                if not first:
                    down(n, s, 2)
                    down(n, s, 3)
                if left > 0:
                    for o in (4, 5, 6):
                        gate_up(n + 1, 1 - s, o)
                if left > 1:
                    transpose_x1(n + 2, s, attn_ps)
                if left > 0:
                    gate_up(n + 1, 1 - s, 7)
                if left > 1:
                    gate_up(n + 2, s, 0)
                    gate_up(n + 2, s, 1)

            pe.wait_ge(pv_free, START + GROUPS * QC)
            pe.wait_ge(mx_copied, GROUPS * QC)
            for k in range(2):
                pe.wait_ge(exp_done[k], GROUPS * QC * EPC // 2)
            phase3(-1, 1, CHUNKS, True)
            with pe.Fori(0, CHUNKS // 2 - 1) as i:
                for s in range(2):
                    phase3(2 * i + s, s, 2)
            for s in range(2):
                phase3(CHUNKS - 2 + s, s, 1 - s)

        @block.scalar
        def _(act):
            def x_high(n, i, s):
                act.wait_ge(x_loaded[s], 16 * (i + 1))
                nc.scalar.activation(x_hi[s][:, :, :], x_raw[:, s, :, :], ACT.Copy).then_inc(x_hi_done, 1)

            x_high(0, 0, 0)
            for n in range(3):
                act.wait_ge(w_loaded[n], 16)
                nc.scalar.activation(w_hi[:, :, w_piece[n]], w_raw[:, :, w_piece[n]], ACT.Copy)\
                  .then_inc(w_hi_done, 1)
            x_high(1, 0, 1)

            def y_high(m):
                act.wait_ge(y_normed, m + 1)
                nc.scalar.activation(y_hi[:, :, :], y_n[:, :, :], ACT.Copy).then_inc(y_hi_done, 1)

            def exps(t, rt, last=False, heads=range(G)):
                for h in heads:
                    act.wait_ge(score_full, START + G * t + h + 1)
                    nc.scalar.activation(probs[:, rt % 2, h, :], score_bank(rt, h, last), ACT.Exp, scale=SCALE)\
                      .then_inc(exp_done[h % 2], 1)

            def phase1(i, last):
                for s in range(2):
                    n = 2 * i + s

                    def high_plain(side):
                        a, b = 2 * side + 1, 4 * side + 2
                        act.wait_ge(proj_done, 8 * n + b + 1)
                        act.wait_ge(parts_stored[a], START + PARTS_STORE * n)
                        nc.scalar.activation(parts[:, a, 0, :], p1_bank[b], ACT.Copy).then_inc(hi_done[a], 1)

                    def high_rotated(side):
                        a = 2 * side
                        act.wait_ge(rope_added[side], START + n + 1)
                        act.wait_ge(parts_stored[a], START + PARTS_STORE * n)
                        nc.scalar.activation(parts[:, a, 0, :], roped[:, side, :], ACT.Copy)\
                          .then_inc(hi_done[a], 1)

                    def copy_v(v):
                        act.wait_ge(proj_done, 8 * n + 4 * (v + 1))
                        for t in range(2):
                            ins = nc.scalar.activation(
                                v_all[:, ds(i, 1), :, s * TPC + 2 * v + t, :].rearrange("p a g d -> p (a g) d"),
                                p1_bank[4 * v + 3][:, t * C:(t + 1) * C].rearrange("p (g d) -> p g d", g=GPB), ACT.Copy)
                        ins.then_inc(v_copied[v], 1)

                    def middle(a):
                        act.wait_ge(rest_done[a], START + n + 1)
                        nc.scalar.activation(parts[:, a, 1, :], rest[:, a, :], ACT.Copy).then_inc(mid_done[a], 1)

                    high_plain(0)
                    middle(1)
                    copy_v(0)
                    high_rotated(0)
                    middle(0)
                    high_plain(1)
                    middle(3)
                    copy_v(1)
                    if last and s == 1:
                        exps(0, 0, heads=(0, 1))
                    high_rotated(1)
                    if last and s == 1:
                        exps(0, 0, heads=(2, 3))
                    middle(2)
                    if not last:
                        act.wait_ge(proj_done, 8 * n + 8)
                        x_high(n + 2, i + 1, s)

            with act.Fori(0, BATCH - 1) as i:
                phase1(i, False)
            phase1(BATCH - 1, True)

            def x1t_high(m, s, src):
                act.wait_ge(b_done, m + 1)
                nc.scalar.activation(x1t_hi[s][:, :, :], src.rearrange("p (k t) -> p k t", k=KC), ACT.Copy)\
                  .then_inc(x1t_hi_done, 1)

            def copy_o(i, k):
                act.wait_ge(pv_done, START + KT * (4 * i + k + 1))
                act.wait_ge(o_stored[k % 2], START + O_STORE * (2 * i + k // 2))
                nc.scalar.activation(o_sb[:, k % 2, :], pv[k % 2], ACT.Copy).then_inc(pv_free, 1)

            exps(1, 1)

            def phase2(i, last):
                for j in range(1, STEPS + 1):
                    t = STEPS * i + j
                    if not (last and j >= STEPS - 1):
                        act.wait_ge(pv_done, START + t)
                        exps(t + 1, j + 1, last)
                    if last and j == Y0_STEP:
                        y_high(0)
                    if last and j == X1T0_STEP + 1:
                        x1t_high(0, 0, x1t0_ps)
                    if j % KT == 0:
                        copy_o(i, j // KT - 1)

            with act.Fori(0, BODIES - 1) as i:
                phase2(i, False)
            phase2(BODIES - 1, True)

            def silu_gate(n, o):
                act.wait_ge(g_full, OT * n + o + 1)
                act.wait_ge(fused_done[o % 2], START + OT // 2 * n + o // 2)
                nc.scalar.activation(silu[:, o % 2, :], g_ps[o % 2], ACT.Silu, scale=sg_sb[:, o:o + 1])\
                  .then_inc(silu_done[o % 2], 1)

            def fused_high(n, s, o):
                act.wait_ge(fused_done[o % 2], START + OT // 2 * n + o // 2 + 1)
                nc.scalar.activation(f_hi[s][:, o, :], fused[:, o % 2, :], ACT.Copy).then_inc(f_hi_done, 1)

            def store_out(n):
                act.wait_ge(ffn_loaded, 16 * 7)
                act.wait_ge(out_ready, START + TPC * (n + 1))
                act.dma_start(out[ds(n * CH, CH), :].rearrange("(t p) c -> p t c", p=P), out_sb[:, :, :])\
                  .then_inc(out_stored, 16)

            act.wait_ge(ffn_loaded, 16 * 7)
            y_high(1)
            for o in (0, 1):
                silu_gate(0, o)
                fused_high(0, 0, o)

            def phase3(n, s, left, first=False):
                if left > 0:
                    for o in (2, 3, 4):
                        silu_gate(n + 1, o)
                        fused_high(n + 1, 1 - s, o)
                    silu_gate(n + 1, 5)
                    silu_gate(n + 1, 6)
                    fused_high(n + 1, 1 - s, 5)
                if left > 1:
                    x1t_high(n + 2, s, attn_ps)
                if left > 0:
                    fused_high(n + 1, 1 - s, 6)
                    silu_gate(n + 1, 7)
                    fused_high(n + 1, 1 - s, 7)
                if left > 1:
                    act.wait_ge(d_done, START + 2 * (n + 1))
                    for o in (0, 1):
                        silu_gate(n + 2, o)
                        fused_high(n + 2, s, o)
                if left > 2:
                    y_high(n + 3)
                if not first:
                    store_out(n)

            phase3(-1, 1, CHUNKS, True)
            with act.Fori(0, CHUNKS // 2 - 2) as i:
                for s in range(2):
                    phase3(2 * i + s, s, 3)
            for n in range(CHUNKS - 4, CHUNKS - 1):
                phase3(n, n % 2, CHUNKS - 1 - n)
            n = CHUNKS - 1
            for half in range(2):
                act.wait_ge(out_ready, START + TPC * n + 2 * (half + 1))
                rows = slice(n * CH + 2 * P * half, n * CH + 2 * P * (half + 1))
                act.dma_start(out[rows, :].rearrange("(t p) c -> p t c", p=P), out_sb[:, 2 * half:2 * half + 2, :])\
                  .then_inc(out_stored, 16)
            act.wait_ge(out_stored, START + 16 * (CHUNKS + 1))

        @block.vector
        def _(dve):
            nc.vector.memset(k_stack[0][STACK:SHIFT, :, :], 1.0).then_inc(ones_done, 1)

            for n in range(3):
                dve.wait_ge(w_hi_done, n + 1)
                nc.vector.tensor_tensor(w_lo[:, :, w_piece[n]], w_raw[:, :, w_piece[n]],
                                        w_hi[:, :, w_piece[n]].bitcast(fp32), ALU.subtract).then_inc(w_lo_done, 1)
                if n == 0:
                    nc.vector.memset(v_ones[0][:, :, :, :], 1.0).then_inc(ones_done, 1)
            dve.wait_ge(tables_loaded, 32)

            def row_max(i, r):
                dve.wait_ge(mscore_full, 2 * MPG * i + r + 1)
                nc.vector.tensor_reduce(out=mx[:, (r // MPC) % 2, r % MPC:r % MPC + 1], in_=mscore[r % 2],
                                        axis=AX.X, op=ALU.max).then_inc(mscore_free[r % 2], 1)

            def split_max_first(c, rc):
                for k in range(2):
                    dve.wait_ge(mscore_free[k], MPC // 2 * (c + 1))
                nc.vector.tensor_scalar(mx_part[0], mx[:, rc % 2, :], -1.0, None, ALU.mult).then_inc(mx_step, 1)

            def split_max(c, rc):
                dve.wait_ge(mx_step, 3 * c + 1)
                nc.vector.scalar_tensor_tensor(out=mx_rest[:, :], in0=mx[:, rc % 2, :], scalar=-1.0,
                                               in1=mx_part[0], op0=ALU.mult, op1=ALU.subtract)\
                  .then_inc(mx_step, 1)
                dve.wait_ge(mx_step, 3 * c + 2)
                nc.vector.tensor_copy(mx_part[1], mx_rest[:, :]).then_inc(mx_step, 1)
                dve.wait_ge(mx_step, 3 * c + 3)
                nc.vector.tensor_tensor(mx_part[2], mx_rest[:, :], mx_part[1], ALU.subtract)\
                  .then_inc(mx_split, 1)

            def copy_rows(c, src):
                dve.wait_ge(mx_transposed, c + 1)
                dve.wait_ge(shift_loaded, SHIFT_LOAD * c)
                nc.vector.tensor_copy(mx_rows[:, :], src[0:PARTS * MPC, 0:P]).then_inc(mx_copied, 1)

            def phase1(i, maxima=(None, None)):
                for s in range(2):
                    n = 2 * i + s
                    cols = slice(s * CH, (s + 1) * CH)

                    def rope(side):
                        b = 4 * side
                        dve.wait_ge(proj_done, 8 * n + b + 2)
                        dve.wait_ge(rope_added[side], START + n)
                        nc.vector.tensor_tensor(rope_a[:, side, :], p1_bank[b], cos_sb[:, cols], ALU.mult)\
                          .then_inc(proj_read[b], 1)
                        nc.vector.tensor_tensor(rope_r[:, side, :], p1_bank[b + 1], sin_sb[:, cols], ALU.mult)\
                          .then_inc(proj_read[b + 1], 1)

                    def take_rest(a):
                        dve.wait_ge(hi_done[a], n + 1)
                        dve.wait_ge(lo_done[a], START + n)
                        src = p1_bank[4 * (a // 2) + 2] if a % 2 else roped[:, a // 2, :]
                        nc.vector.tensor_tensor(rest[:, a, :], src, parts[:, a, 0, :], ALU.subtract)\
                          .then_inc(rest_done[a], 1)

                    def maximum(k):
                        if maxima[s] is not None:
                            r = maxima[s] + k
                            row_max(0, r)
                            if r == FIRST_T:
                                copy_rows(0, first_mx_t)
                            if r == MPC - 1:
                                split_max_first(0, 0)
                            if r == MPC:
                                split_max(0, 0)

                    maximum(0)
                    rope(0)
                    maximum(1)
                    take_rest(1)
                    maximum(2)
                    maximum(3)
                    take_rest(0)
                    maximum(4)
                    rope(1)
                    maximum(5)
                    take_rest(3)
                    maximum(6)
                    maximum(7)
                    take_rest(2)

            with dve.Fori(0, BATCH - 2) as i:
                phase1(i)
            nc.vector.memset(mx_parts[:, PARTS * MPC:P], 0.0)
            phase1(BATCH - 2, (None, 0))
            phase1(BATCH - 1, (LEAD // 3, 2 * LEAD // 3))

            def invert(b):
                dve.wait_ge(sums_loaded[b // 3], 16 * (3 if b < 3 else 1))
                nc.vector.reciprocal(sums_sb[:, b, :], sums_sb[:, b, :]).then_inc(rinv_done, 1)

            def phase2(i, last):
                for j in range(STEPS):
                    more = not (last and j // KT == STEPS // KT - 1)
                    c = j // KT + 1
                    for r in (2 * j + LEAD, 2 * j + LEAD + 1):
                        if not (last and r >= 2 * MPG):
                            row_max(i, r)
                        if j % KT == 4 and more:
                            if r % 2 == 0:
                                split_max_first(4 * i + c, c)
                            else:
                                split_max(4 * i + c, c)
                        if j % KT == 5 and more and r % 2 == 0:
                            copy_rows(4 * i + c, pv[c % 2].bitcast(bf16))
                    if last and j in INVERT_STEPS:
                        invert(INVERT_STEPS.index(j))

            with dve.Fori(0, BODIES - 1) as i:
                phase2(i, False)
            phase2(BODIES - 1, True)

            def moments(m, k, step, steps, src, tiles=slice(0, TPC)):
                for t in range(TPC)[tiles]:
                    ins = nc.vector.bn_stats(st[:, k, t, :], src[:, t, :])
                ins.then_inc(ln_step[k], 1)
                dve.wait_ge(ln_step[k], steps * m + step + 1)
                mean_e, dev_e, mean_o, dev_o = (st[:, k, tiles, c] for c in (1, 2, 4, 5))
                mean, diff, dev = (x[:, k, tiles] for x in (ln_mean, ln_diff, ln_dev))
                nc.vector.tensor_tensor(mean, mean_e, mean_o, ALU.add)
                nc.vector.tensor_tensor(diff, mean_e, mean_o, ALU.subtract)
                nc.vector.tensor_tensor(dev, dev_e, dev_o, ALU.add).then_inc(ln_step[k], 1)
                dve.wait_ge(ln_step[k], steps * m + step + 2)
                nc.vector.tensor_scalar(mean, mean, 0.5, None, ALU.mult)
                nc.vector.tensor_scalar(dev, dev, 1.0 / C, EPS, ALU.mult, ALU.add)
                nc.vector.scalar_tensor_tensor(out=diff, in0=diff, scalar=0.25, in1=diff,
                                               op0=ALU.mult, op1=ALU.mult).then_inc(ln_step[k], 1)
                dve.wait_ge(ln_step[k], steps * m + step + 3)
                nc.vector.tensor_tensor(var_eps[:, k, tiles], dev, diff, ALU.add).then_inc(var_ready[k], 1)

            def normalise(m, k, src, dst, done, tiles=slice(0, TPC)):
                dve.wait_ge(rstd_ready[k], m + 1)
                for t in range(TPC)[tiles]:
                    ins = nc.vector.tensor_scalar(dst[:, t, :], src[:, t, :], ln_mean[:, k, t:t + 1],
                                                  rstd[:, k, t:t + 1], ALU.subtract, ALU.mult)
                    if k == 1 or t == TPC - 1:
                        ins.then_inc(done, 1)

            def moments1(m, src=attn_ps):
                dve.wait_ge(a_done, m + 1)
                dve.wait_ge(x_in_loaded, 16 * (m + 1))
                nc.vector.tensor_tensor(res1[:, :, :], src.rearrange("p (t c) -> p t c", c=C), x_in[:, :, :],
                                        ALU.add).then_inc(attn_read, 1)
                dve.wait_ge(attn_read, m + 1)
                moments(m, 0, 0, 3, res1)

            def scale_down(m):
                dve.wait_ge(out_ready, START + TPC * m)
                dve.wait_ge(d_done, START + 2 * (m + 1))
                nc.vector.tensor_tensor(res2[:, :, :], down_ps.rearrange("p (t c) -> p t c", c=C),
                                        sd_sb[:, :].unsqueeze(1).to_broadcast([P, TPC, C]), ALU.mult)\
                  .then_inc(down_read, 1)

            def add_x1(m, s):
                dve.wait_ge(down_read, START + m + 1)
                nc.vector.tensor_tensor(res2[:, :, :], res2[:, :, :], x1[s][:, :, :], ALU.add)\
                  .then_inc(ln_step[1], 1)

            def moments2(m):
                dve.wait_ge(ln_step[1], 4 * m + 1)
                moments(m, 1, 1, 4, res2)

            def fuse(n, o):
                dve.wait_ge(u_full, OT * n + o + 1)
                dve.wait_ge(silu_done[o % 2], START + OT // 2 * n + o // 2 + 1)
                dve.wait_ge(f_lo_done[o % 2], START + OT // 2 * n + o // 2)
                nc.vector.scalar_tensor_tensor(out=fused[:, o % 2, :], in0=u_ps[o % 2], scalar=su_sb[:, o:o + 1],
                                               in1=silu[:, o % 2, :], op0=ALU.mult, op1=ALU.mult)\
                  .then_inc(fused_done[o % 2], 1)

            def x1t_low(m, s, src=attn_ps):
                dve.wait_ge(x1t_hi_done, m + 1)
                nc.vector.tensor_tensor(x1t_lo[s][:, :, :], src.rearrange("p (k t) -> p k t", k=KC),
                                        x1t_hi[s][:, :, :].bitcast(fp32), ALU.subtract).then_inc(x1t_ready, 1)

            dve.wait_ge(ffn_loaded, 16 * 7)
            moments1(0, attn0_ps)
            normalise(0, 0, res1, x1[0], x1_ready)
            x1t_low(0, 0, x1t0_ps)
            fuse(0, 0)
            fuse(0, 1)

            def phase3(n, s, left, first=False):
                if left > 0:
                    fuse(n + 1, 2)
                    fuse(n + 1, 3)
                if left > 1:
                    moments1(n + 2)
                if not first:
                    scale_down(n)
                if left > 0:
                    fuse(n + 1, 4)
                if not first:
                    add_x1(n, s)
                if left > 1:
                    if not first:
                        dve.wait_ge(ln_step[1], 4 * n + 1)
                    normalise(n + 2, 0, res1, x1[s], x1_ready)
                if left > 0:
                    fuse(n + 1, 5)
                    fuse(n + 1, 6)
                if left > 1:
                    x1t_low(n + 2, s)
                if left > 0:
                    fuse(n + 1, 7)
                if first:
                    invert(BATCH - 1)
                else:
                    moments2(n)
                if left > 1:
                    fuse(n + 2, 0)
                    fuse(n + 2, 1)
                if not first:
                    dve.wait_ge(out_stored, START + 16 * n)
                    normalise(n, 1, res2, out_sb, out_ready)

            phase3(-1, 1, CHUNKS, True)
            with dve.Fori(0, CHUNKS // 2 - 1) as i:
                for s in range(2):
                    phase3(2 * i + s, s, 2)
            phase3(CHUNKS - 2, 0, 1)
            n = CHUNKS - 1
            dve.wait_ge(out_ready, START + TPC * n)
            for half in range(2):
                tiles = slice(2 * half, 2 * half + 2)
                dve.wait_ge(d_done, START + 2 * n + half + 1)
                nc.vector.tensor_tensor(res2[:, tiles, :],
                                        down_ps[:, half * NB:(half + 1) * NB].rearrange("p (t c) -> p t c", c=C),
                                        sd_sb[:, :].unsqueeze(1).to_broadcast([P, 2, C]), ALU.mult)\
                  .then_inc(down_read, 1)
                dve.wait_ge(down_read, START + n + half + 1)
                nc.vector.tensor_tensor(res2[:, tiles, :], res2[:, tiles, :], x1[1][:, tiles, :], ALU.add)\
                  .then_inc(ln_step[1], 1)
                dve.wait_ge(ln_step[1], 4 * (n + half) + 1)
                moments(n + half, 1, 1, 4, res2, tiles)
                if half == 0:
                    dve.wait_ge(out_stored, START + 16 * n)
                normalise(n + half, 1, res2, out_sb, out_ready, tiles)

        @block.gpsimd
        def _(pool):
            for count in from_start:
                pool.sem_inc(count, START)
            nc.gpsimd.memset(ident_f[:, :], 0.0).then_inc(ident0, 1)
            nc.gpsimd.memset(ident_b[:, :], 0.0).then_inc(ident0, 1)
            nc.gpsimd.memset(neg_half[:, :], -0.5).then_inc(ident0, 1)
            pool.wait_ge(ident0, 3)
            nc.gpsimd.affine_select(out=ident_f[:, :], in_=ident_f[:, :], compare_op=ALU.not_equal, fill=1.0,
                                    base=0, pattern=[[-1, P]], channel_multiplier=1).then_inc(consts_done, 1)
            nc.gpsimd.affine_select(out=ident_b[:, :], in_=ident_b[:, :], compare_op=ALU.not_equal, fill=1.0,
                                    base=0, pattern=[[-1, P]], channel_multiplier=1).then_inc(consts_done, 1)

            def x_low(n, s):
                pool.wait_ge(x_hi_done, n + 1)
                nc.gpsimd.tensor_tensor(x_lo[s][:, :, :], x_raw[:, s, :, :], x_hi[s][:, :, :].bitcast(fp32),
                                        ALU.subtract).then_inc(x_lo_done, 1)

            def place_v(b, hg, p):
                nc.gpsimd.tensor_copy(
                    v_ones[p][:, :, :, 0:HD],
                    v_all[:, ds(b, 1), ds(hg, 1), :, :].rearrange("p a b k (h d) -> p (a b k) h d", d=HD))\
                  .then_inc(v_ready, 1)

            x_low(0, 0)

            def phase1(i, last):
                for s in range(2):
                    n = 2 * i + s

                    def add_rope(side):
                        pool.wait_ge(proj_read[4 * side], START + n + 1)
                        pool.wait_ge(proj_read[4 * side + 1], START + n + 1)
                        pool.wait_ge(rest_done[2 * side], START + n)
                        nc.gpsimd.tensor_tensor(roped[:, side, :], rope_a[:, side, :], rope_r[:, side, :],
                                                ALU.add).then_inc(rope_added[side], 1)

                    def low(a):
                        pool.wait_ge(mid_done[a], n + 1)
                        nc.gpsimd.tensor_tensor(parts[:, a, 2, :], rest[:, a, :], parts[:, a, 1, :],
                                                ALU.subtract).then_inc(lo_done[a], 1)

                    add_rope(0)
                    if not (last and s == 1):
                        x_low(n + 1, 1 - s)
                    if last and s == 0:
                        for v in range(2):
                            pool.wait_ge(v_copied[v], START + QC)
                        pool.wait_ge(ones_done, 2)
                        place_v(0, 0, 0)
                    low(1)
                    low(0)
                    add_rope(1)
                    low(3)
                    low(2)

            with pool.Fori(0, BATCH - 1) as i:
                phase1(i, False)
            phase1(BATCH - 1, True)

            pool.wait_ge(lo_done[2], START + CHUNKS)

            pool.wait_ge(v_ready, 1)
            nc.gpsimd.memset(v_ones[1][:, :, :, :], 1.0).then_inc(ones_done, 1)
            pool.wait_ge(ones_done, 3)
            nc.gpsimd.memset(k_stack[1][STACK:SHIFT, :, :], 1.0).then_inc(ones_done, 1)
            pool.wait_ge(ones_done, 4)
            pool.wait_ge(ffn_loaded, 16 * 7)
            for w, n, k in ((wg_sb, 0, KC), (wu_sb, 1, KC), (wd_sb, 2, OT)):
                nc.gpsimd.tensor_copy(w[:, :, :], w8_sb[:, n, :].bitcast(i8).rearrange("p (k o) -> p k o", k=k))\
                  .then_inc(ffn_cast, 1)
            nc.gpsimd.tensor_copy(wo_hi[:, :, :], wo_sb[:, :, :]).then_inc(wo_split, 1)
            pool.wait_ge(wo_split, 1)
            nc.gpsimd.tensor_tensor(wo_lo[:, :, :], wo_sb[:, :, :], wo_hi[:, :, :].bitcast(fp32), ALU.subtract)\
              .then_inc(wo_split, 1)

            def phase2(i, last):
                g = 2 * i + 1
                pool.wait_ge(ones_done, 4)
                pool.wait_ge(pv_done, START + STEPS * i)
                place_v(g // GPB, g % GPB, 1)
                if not last:
                    g = 2 * i + 2
                    pool.wait_ge(ones_done, 4)
                    pool.wait_ge(pv_done, START + STEPS * i + STEPS // 2)
                    place_v(g // GPB, g % GPB, 0)

            with pool.Fori(0, BODIES - 1) as i:
                phase2(i, False)
            phase2(BODIES - 1, True)

            pool.wait_ge(ident0, 3)

            def norm_y(m):
                pool.wait_ge(y_loaded, Y_LOAD * (m + 1))
                pool.wait_ge(a_done, m)
                nc.gpsimd.tensor_tensor(y_n[:, :, :], y_in[:, :, :], r_in[:, :, :], ALU.mult).then_inc(y_normed, 1)

            def root(m, k):
                pool.wait_ge(var_ready[k], m + 1)
                nc.gpsimd.tensor_tensor(rstd[:, k, :], var_eps[:, k, :], neg_half[:, :], ALU.pow)\
                  .then_inc(rstd_ready[k], 1)

            def fused_low(n, s, tiles):
                for o in tiles:
                    pool.wait_ge(f_hi_done, OT * n + o + 1)
                    nc.gpsimd.tensor_tensor(f_lo[s][:, o, :], fused[:, o % 2, :],
                                            f_hi[s][:, o, :].bitcast(fp32), ALU.subtract)\
                      .then_inc(f_lo_done[o % 2], 1)

            def y_low(m):
                pool.wait_ge(y_hi_done, m + 1)
                nc.gpsimd.tensor_tensor(y_lo[:, :, :], y_n[:, :, :], y_hi[:, :, :].bitcast(fp32), ALU.subtract)\
                  .then_inc(y_lo_done, 1)

            norm_y(0)
            y_low(0)
            root(0, 0)
            norm_y(1)
            y_low(1)
            fused_low(0, 0, (0,))

            def phase3(n, s, left, first=False):
                if left > 0:
                    fused_low(n + 1, 1 - s, (1, 2, 3))
                if left > 1:
                    root(n + 2, 0)
                if left > 0:
                    fused_low(n + 1, 1 - s, (4, 5, 6, 7))
                if not first:
                    root(n, 1)
                if left > 2:
                    norm_y(n + 3)
                if left > 1:
                    fused_low(n + 2, s, (0,))
                if left > 2:
                    y_low(n + 3)

            phase3(-1, 1, CHUNKS, True)
            with pool.Fori(0, CHUNKS // 2 - 2) as i:
                for s in range(2):
                    phase3(2 * i + s, s, 3)
            for n in range(CHUNKS - 4, CHUNKS - 1):
                phase3(n, n % 2, CHUNKS - 1 - n)
            for half in range(2):
                pool.wait_ge(var_ready[1], CHUNKS + half)
                tiles = slice(2 * half, 2 * half + 2)
                nc.gpsimd.tensor_tensor(rstd[:, 1, tiles], var_eps[:, 1, tiles], neg_half[:, tiles], ALU.pow)\
                  .then_inc(rstd_ready[1], 1)


def kernel(**inputs):
    import numpy as np
    import concourse.bacc as bacc
    from concourse import mybir
    from concourse.bass_utils import run_bass_kernel_spmd

    HEADS, HD, HALF, T = 16, 16, 8, 1024
    x = np.asarray(inputs["L0_attn_x"])
    B, _, C = x.shape
    x_nat = np.ascontiguousarray(x.reshape(B * T, C))
    heads = np.arange(HEADS)[:, None] * HD
    d = np.arange(HALF)[None, :]
    rotary = (heads + d).ravel()
    partner = (heads + (d + HALF // 2) % HALF).ravel()
    plain = (heads + HALF + d).ravel()
    wq, wk, wv, wo = (np.asarray(inputs[f"L0_attn_{n}"]) for n in ("wq", "wk", "wv", "wo"))
    w_qkv = np.ascontiguousarray(np.concatenate(
        [wq.T[:, rotary], wq.T[:, partner], wq.T[:, plain],
         wk.T[:, rotary], wk.T[:, partner], wk.T[:, plain], wv.T], axis=1))
    inv_freq = (1.0 / np.float32(10000.0) ** (np.arange(0, HD, 2, dtype=np.float32) / np.float32(HD))).astype(np.float32)
    angle = inv_freq[:, None] * np.arange(T, dtype=np.float32)[None, :]
    sign = np.where(np.arange(HALF) < HALF // 2, -1.0, 1.0).astype(np.float32)[:, None]
    cos = np.tile(np.cos(angle), (HEADS, 1)).astype(np.float32)
    sin = np.tile(sign * np.sin(angle), (HEADS, 1)).astype(np.float32)
    arrays = {
        "x_nat": x_nat,
        "x_cols": np.ascontiguousarray(x_nat.T),
        "w_qkv": w_qkv,
        "w_out": np.ascontiguousarray(wo.T),
        "rope_cos": cos,
        "rope_sin": sin,
    }
    for name in ("w_gate", "w_up", "w_down", "s_gate", "s_up", "s_down"):
        arrays[name] = np.ascontiguousarray(np.asarray(inputs[f"L0_ffn_{name}"]))
    for name in ("w_gate", "w_up", "w_down"):
        arrays[name] = arrays[name].view(np.int32)
    for name in ("s_gate", "s_up"):
        arrays[name] = np.ascontiguousarray(arrays[name].reshape(-1, 128).T)
    nc = bacc.Bacc("TRN2", target_bir_lowering=False, num_devices=1)
    args = [nc.dram_tensor(n, a.shape, mybir.dt.from_np(a.dtype), kind="ExternalInput").ap()
            for n, a in arrays.items()]
    out = nc.dram_tensor("out", (B * T, C), mybir.dt.float32, kind="ExternalOutput").ap()
    build_attention_ffn_block(nc, *args, out)
    r = run_bass_kernel_spmd(nc, [arrays], core_ids=[0])
    return r.results[0]["out"].reshape(B, T, C)
```
